# Optimizing a Trainium2 kernel written in Bass

```python
import numpy as np
import jax
import jax.numpy as jnp

def _softmax(x, axis=-1):
    return jax.nn.softmax(x, axis=axis)

def _gelu(x):
    return jax.nn.gelu(x, approximate=True)

def _silu(x):
    return jax.nn.silu(x)

def _sigmoid(x):
    return jax.nn.sigmoid(x)

def _layernorm(x, axis=-1, eps=1e-05):
    m = jnp.mean(x, axis=axis, keepdims=True)
    v = jnp.var(x, axis=axis, keepdims=True)
    return (x - m) / jnp.sqrt(v + eps)

def _scatter_add(tgt, idx, src, axis=0):
    return tgt.at[idx].add(src)

def _segment_sum(src, seg, n):
    return jax.ops.segment_sum(src, seg, n)
kernel_name = 'mk_decoder_preln_d1_seqx_r8_0a7ec4'

def setup_inputs(seed: int=0):
    np.random.seed(seed)
    _w = jnp.asarray

    def _rec_inputs():
        import jax
        import jax.numpy as jnp
        _rk = jax.random.key(seed)
        x = -0.0002928 + 1 * jax.random.normal(jax.random.fold_in(_rk, 1), (8, 256, 256), jnp.float32)
        _lenS = 256 - jax.random.randint(jax.random.fold_in(_rk, 7), (8,), 0, max(1, 256 // 4) + 1, jnp.int32)
        _lenS2 = 64 - jax.random.randint(jax.random.fold_in(_rk, 8), (8,), 0, max(1, 64 // 4) + 1, jnp.int32)
        _ctx_2048P = jax.random.normal(jax.random.fold_in(_rk, 11), (8, 16, 256), jnp.float32)
        _ctx_2048c = jax.random.dirichlet(jax.random.fold_in(_rk, 511), 0.3 * jnp.ones((16,), jnp.float32), (8, 64))
        _ctx_2048t = jnp.einsum('bsk,bkd->bsd', _ctx_2048c, _ctx_2048P)
        _ctx_2048t = _ctx_2048t * jax.lax.rsqrt(jnp.mean(jnp.square(_ctx_2048t)) + 1e-12) * 0.953939
        ctx_2048 = 4.13588e-05 + 0.999923 * (_ctx_2048t + 0.3 * jax.random.normal(jax.random.fold_in(_rk, 611), (8, 64, 256), jnp.float32))
        _validS = jnp.arange(256)[None, :] < _lenS[:, None]
        _validS2 = jnp.arange(64)[None, :] < _lenS2[:, None]
        _causal = jnp.tril(jnp.ones((256, 256), dtype=bool))
        mask_1xSxS2_ff0 = jnp.where(jnp.ones((1, 256, 64), dtype=bool), 0.0, -1000000000.0).astype(jnp.float32)
        return (x, ctx_2048, mask_1xSxS2_ff0)
    x, ctx_2048, mask_1xSxS2_ff0 = _rec_inputs()

    def _L0_attn_setup():
        import jax, jax.numpy as jnp
        import numpy as np
        from jax import lax
        HID = 256
        NH = 64
        P = 64
        N = 128
        G = 1
        CS = 32
        K = 4
        D_INNER = NH * P
        CONV_DIM = D_INNER + 2 * G * N
        PROJ = D_INNER + CONV_DIM + NH
        EPS = 1e-05
        BATCH, SEQ = (2, 256)

        def _segsum(x):
            T = x.shape[-1]
            xc = jnp.cumsum(x, axis=-1)
            seg = xc[..., :, None] - xc[..., None, :]
            mask = jnp.tril(jnp.ones((T, T), dtype=bool))
            return jnp.where(mask, seg, -jnp.inf)

        def _mamba2_forward(hidden_states, W_in, conv_w, conv_b, dt_bias, A_log, D_param, norm_w, W_out):
            B_, L_ = hidden_states.shape[:2]
            proj = hidden_states @ W_in.T
            z = proj[..., :D_INNER]
            xBC = proj[..., D_INNER:D_INNER + CONV_DIM]
            dt = proj[..., D_INNER + CONV_DIM:]
            xc = lax.conv_general_dilated(jnp.transpose(xBC, (0, 2, 1)), conv_w, window_strides=(1,), padding=[(K - 1, 0)], feature_group_count=CONV_DIM)
            xc = xc + conv_b[None, :, None]
            xBC = jax.nn.silu(jnp.transpose(xc, (0, 2, 1)))
            x = xBC[..., :D_INNER].reshape(B_, L_, NH, P)
            Bm = xBC[..., D_INNER:D_INNER + G * N].reshape(B_, L_, G, N)
            Cm = xBC[..., D_INNER + G * N:].reshape(B_, L_, G, N)
            dt = jax.nn.softplus(dt + dt_bias)
            A = -jnp.exp(A_log)
            Bh = jnp.repeat(Bm, NH // G, axis=2)
            Ch = jnp.repeat(Cm, NH // G, axis=2)
            nc = L_ // CS
            x_dt = (x * dt[..., None]).reshape(B_, nc, CS, NH, P)
            B_c = Bh.reshape(B_, nc, CS, NH, N)
            C_c = Ch.reshape(B_, nc, CS, NH, N)
            dA = jnp.transpose((dt * A).reshape(B_, nc, CS, NH), (0, 3, 1, 2))
            A_cum = jnp.cumsum(dA, axis=-1)
            Lmat = jnp.exp(_segsum(dA))
            Y_diag = jnp.einsum('bclhn,bcshn,bhcls,bcshp->bclhp', C_c, B_c, Lmat, x_dt)
            decay_states = jnp.exp(A_cum[..., -1:] - A_cum)
            states = jnp.einsum('bclhn,bhcl,bclhp->bchpn', B_c, decay_states, x_dt)
            da_last = A_cum[..., -1]

            def step(prev, inp):
                s_k, d_k = inp
                new = prev * jnp.exp(d_k)[..., None, None] + s_k
                return (new, prev)
            _, prev_states = lax.scan(step, jnp.zeros((B_, NH, P, N), dtype=x.dtype), (jnp.transpose(states, (1, 0, 2, 3, 4)), jnp.transpose(da_last, (2, 0, 1))))
            prev_states = jnp.transpose(prev_states, (1, 2, 0, 3, 4))
            Y_off = jnp.einsum('bclhn,bhcpn,bhcl->bclhp', C_c, prev_states, jnp.exp(A_cum))
            y = (Y_diag + Y_off).reshape(B_, L_, NH, P) + D_param[None, None, :, None] * x
            y = y.reshape(B_, L_, D_INNER)
            g = y * jax.nn.silu(z)
            gs = D_INNER // G
            gr = g.reshape(B_, L_, G, gs)
            var = jnp.mean(gr * gr, axis=-1, keepdims=True)
            gn = (gr * lax.rsqrt(var + EPS)).reshape(B_, L_, D_INNER) * norm_w
            return gn @ W_out.T
        key = jax.random.key(seed)
        ks = jax.random.split(key, 8)
        hidden_states = jax.random.normal(ks[0], (BATCH, SEQ, HID), dtype=jnp.float32)
        W_in = jax.random.normal(ks[1], (PROJ, HID), dtype=jnp.float32) * 0.02
        conv_w = jax.random.normal(ks[2], (CONV_DIM, 1, K), dtype=jnp.float32) * 0.2
        conv_b = jax.random.normal(ks[3], (CONV_DIM,), dtype=jnp.float32) * 0.02
        dt = jnp.exp(jax.random.uniform(ks[4], (NH,)) * (np.log(0.1) - np.log(0.001)) + np.log(0.001))
        dt_bias = (dt + jnp.log(-jnp.expm1(-dt))).astype(jnp.float32)
        A_log = jnp.log(jnp.arange(1, NH + 1, dtype=jnp.float32))
        D_param = jnp.ones((NH,), dtype=jnp.float32)
        norm_w = jnp.ones((D_INNER,), dtype=jnp.float32)
        W_out = jax.random.normal(ks[5], (HID, D_INNER), dtype=jnp.float32) * 0.02
        return {'hidden_states': hidden_states, 'W_in': W_in, 'conv_w': conv_w, 'conv_b': conv_b, 'dt_bias': dt_bias, 'A_log': A_log, 'D_param': D_param, 'norm_w': norm_w, 'W_out': W_out}
    _L0_attn_all = _L0_attn_setup()
    _L0_attn_in = {k: v for k, v in _L0_attn_all.items() if k in ('W_in', 'conv_w', 'conv_b', 'dt_bias', 'A_log', 'D_param', 'norm_w', 'W_out')}
    del _L0_attn_all

    def _L0_xattn_setup():
        import jax, jax.numpy as jnp
        import numpy as np
        H = 256
        NH = 16
        NKV = 4
        HD = 128
        GROUPS = NH // NKV
        EPS = 1e-06
        B, S, SE = (1, 256, 512)

        def _rmsnorm(x, w, eps=EPS):
            xf = x.astype(jnp.float32)
            var = jnp.mean(xf * xf, axis=-1, keepdims=True)
            return (xf * jax.lax.rsqrt(var + eps)).astype(x.dtype) * w
        key = jax.random.key(seed)
        ks = jax.random.split(key, 12)
        sc = 0.02
        return {'hidden_states': jax.random.normal(ks[0], (B, S, H), jnp.float32), 'encoder_hidden_states': jax.random.normal(ks[1], (B, SE, H), jnp.float32), 'attention_mask': jnp.zeros((B, S, SE), jnp.float32), 'Wq': jax.random.normal(ks[2], (H, NH * HD), jnp.float32) * sc, 'bq': jax.random.normal(ks[3], (NH * HD,), jnp.float32) * sc, 'Wk': jax.random.normal(ks[4], (H, NKV * HD), jnp.float32) * sc, 'bk': jax.random.normal(ks[5], (NKV * HD,), jnp.float32) * sc, 'Wv': jax.random.normal(ks[6], (H, NKV * HD), jnp.float32) * sc, 'bv': jax.random.normal(ks[7], (NKV * HD,), jnp.float32) * sc, 'Wo': jax.random.normal(ks[8], (NH * HD, H), jnp.float32) * sc, 'qn_w': jnp.ones((HD,), jnp.float32), 'kn_w': jnp.ones((HD,), jnp.float32)}
    _L0_xattn_all = _L0_xattn_setup()
    _L0_xattn_in = {k: v for k, v in _L0_xattn_all.items() if k in ('Wq', 'bq', 'Wk', 'bk', 'Wv', 'bv', 'Wo', 'qn_w', 'kn_w')}
    del _L0_xattn_all

    def _L0_ffn_setup():
        import jax, jax.numpy as jnp
        import numpy as np
        E, TOPK, H, I, NSH = (8, 2, 256, 640, 2)
        B, S = (2, 128)
        key = jax.random.key(seed)
        ks = jax.random.split(key, 8)
        sc = 0.02
        return {'x': jax.random.normal(ks[0], (B, S, H), dtype=jnp.float32), 'w_router': jax.random.normal(ks[1], (E, H), dtype=jnp.float32), 'wg': jax.random.normal(ks[2], (E, I, H), dtype=jnp.float32) * sc, 'wu': jax.random.normal(ks[3], (E, I, H), dtype=jnp.float32) * sc, 'wd': jax.random.normal(ks[4], (E, H, I), dtype=jnp.float32) * sc, 'sg': jax.random.normal(ks[5], (NSH, I, H), dtype=jnp.float32) * sc, 'su': jax.random.normal(ks[6], (NSH, I, H), dtype=jnp.float32) * sc, 'sd': jax.random.normal(ks[7], (NSH, H, I), dtype=jnp.float32) * sc}
    _L0_ffn_all = _L0_ffn_setup()
    _L0_ffn_in = {k: v for k, v in _L0_ffn_all.items() if k in ('w_router', 'wg', 'wu', 'wd', 'sg', 'su', 'sd')}
    del _L0_ffn_all
    return {'x': x, 'ctx_2048': ctx_2048, 'mask_1xSxS2_ff0': mask_1xSxS2_ff0, 'L0_attn_W_in': _L0_attn_in['W_in'], 'L0_attn_conv_w': _L0_attn_in['conv_w'], 'L0_attn_conv_b': _L0_attn_in['conv_b'], 'L0_attn_dt_bias': _L0_attn_in['dt_bias'], 'L0_attn_A_log': _L0_attn_in['A_log'], 'L0_attn_D_param': _L0_attn_in['D_param'], 'L0_attn_norm_w': _L0_attn_in['norm_w'], 'L0_attn_W_out': _L0_attn_in['W_out'], 'L0_xattn_Wq': _L0_xattn_in['Wq'], 'L0_xattn_bq': _L0_xattn_in['bq'], 'L0_xattn_Wk': _L0_xattn_in['Wk'], 'L0_xattn_bk': _L0_xattn_in['bk'], 'L0_xattn_Wv': _L0_xattn_in['Wv'], 'L0_xattn_bv': _L0_xattn_in['bv'], 'L0_xattn_Wo': _L0_xattn_in['Wo'], 'L0_xattn_qn_w': _L0_xattn_in['qn_w'], 'L0_xattn_kn_w': _L0_xattn_in['kn_w'], 'L0_ffn_w_router': _L0_ffn_in['w_router'], 'L0_ffn_wg': _L0_ffn_in['wg'], 'L0_ffn_wu': _L0_ffn_in['wu'], 'L0_ffn_wd': _L0_ffn_in['wd'], 'L0_ffn_sg': _L0_ffn_in['sg'], 'L0_ffn_su': _L0_ffn_in['su'], 'L0_ffn_sd': _L0_ffn_in['sd']}

def reference(x, ctx_2048, mask_1xSxS2_ff0, L0_attn_W_in, L0_attn_conv_w, L0_attn_conv_b, L0_attn_dt_bias, L0_attn_A_log, L0_attn_D_param, L0_attn_norm_w, L0_attn_W_out, L0_xattn_Wq, L0_xattn_bq, L0_xattn_Wk, L0_xattn_bk, L0_xattn_Wv, L0_xattn_bv, L0_xattn_Wo, L0_xattn_qn_w, L0_xattn_kn_w, L0_ffn_w_router, L0_ffn_wg, L0_ffn_wu, L0_ffn_wd, L0_ffn_sg, L0_ffn_su, L0_ffn_sd):
    import jax
    import jax.numpy as jnp

    def _L0_attn_ref(hidden_states, W_in, conv_w, conv_b, dt_bias, A_log, D_param, norm_w, W_out):
        import jax, jax.numpy as jnp
        import numpy as np
        from jax import lax
        HID = 256
        NH = 64
        P = 64
        N = 128
        G = 1
        CS = 32
        K = 4
        D_INNER = NH * P
        CONV_DIM = D_INNER + 2 * G * N
        PROJ = D_INNER + CONV_DIM + NH
        EPS = 1e-05
        BATCH, SEQ = (2, 256)

        def _segsum(x):
            T = x.shape[-1]
            xc = jnp.cumsum(x, axis=-1)
            seg = xc[..., :, None] - xc[..., None, :]
            mask = jnp.tril(jnp.ones((T, T), dtype=bool))
            return jnp.where(mask, seg, -jnp.inf)

        def _mamba2_forward(hidden_states, W_in, conv_w, conv_b, dt_bias, A_log, D_param, norm_w, W_out):
            B_, L_ = hidden_states.shape[:2]
            proj = hidden_states @ W_in.T
            z = proj[..., :D_INNER]
            xBC = proj[..., D_INNER:D_INNER + CONV_DIM]
            dt = proj[..., D_INNER + CONV_DIM:]
            xc = lax.conv_general_dilated(jnp.transpose(xBC, (0, 2, 1)), conv_w, window_strides=(1,), padding=[(K - 1, 0)], feature_group_count=CONV_DIM)
            xc = xc + conv_b[None, :, None]
            xBC = jax.nn.silu(jnp.transpose(xc, (0, 2, 1)))
            x = xBC[..., :D_INNER].reshape(B_, L_, NH, P)
            Bm = xBC[..., D_INNER:D_INNER + G * N].reshape(B_, L_, G, N)
            Cm = xBC[..., D_INNER + G * N:].reshape(B_, L_, G, N)
            dt = jax.nn.softplus(dt + dt_bias)
            A = -jnp.exp(A_log)
            Bh = jnp.repeat(Bm, NH // G, axis=2)
            Ch = jnp.repeat(Cm, NH // G, axis=2)
            nc = L_ // CS
            x_dt = (x * dt[..., None]).reshape(B_, nc, CS, NH, P)
            B_c = Bh.reshape(B_, nc, CS, NH, N)
            C_c = Ch.reshape(B_, nc, CS, NH, N)
            dA = jnp.transpose((dt * A).reshape(B_, nc, CS, NH), (0, 3, 1, 2))
            A_cum = jnp.cumsum(dA, axis=-1)
            Lmat = jnp.exp(_segsum(dA))
            Y_diag = jnp.einsum('bclhn,bcshn,bhcls,bcshp->bclhp', C_c, B_c, Lmat, x_dt)
            decay_states = jnp.exp(A_cum[..., -1:] - A_cum)
            states = jnp.einsum('bclhn,bhcl,bclhp->bchpn', B_c, decay_states, x_dt)
            da_last = A_cum[..., -1]

            def step(prev, inp):
                s_k, d_k = inp
                new = prev * jnp.exp(d_k)[..., None, None] + s_k
                return (new, prev)
            _, prev_states = lax.scan(step, jnp.zeros((B_, NH, P, N), dtype=x.dtype), (jnp.transpose(states, (1, 0, 2, 3, 4)), jnp.transpose(da_last, (2, 0, 1))))
            prev_states = jnp.transpose(prev_states, (1, 2, 0, 3, 4))
            Y_off = jnp.einsum('bclhn,bhcpn,bhcl->bclhp', C_c, prev_states, jnp.exp(A_cum))
            y = (Y_diag + Y_off).reshape(B_, L_, NH, P) + D_param[None, None, :, None] * x
            y = y.reshape(B_, L_, D_INNER)
            g = y * jax.nn.silu(z)
            gs = D_INNER // G
            gr = g.reshape(B_, L_, G, gs)
            var = jnp.mean(gr * gr, axis=-1, keepdims=True)
            gn = (gr * lax.rsqrt(var + EPS)).reshape(B_, L_, D_INNER) * norm_w
            return gn @ W_out.T
        return _mamba2_forward(hidden_states, W_in, conv_w, conv_b, dt_bias, A_log, D_param, norm_w, W_out)

    def _L0_xattn_ref(hidden_states, encoder_hidden_states, attention_mask, Wq, bq, Wk, bk, Wv, bv, Wo, qn_w, kn_w):
        import jax, jax.numpy as jnp
        import numpy as np
        H = 256
        NH = 16
        NKV = 4
        HD = 128
        GROUPS = NH // NKV
        EPS = 1e-06
        B, S, SE = (1, 256, 512)

        def _rmsnorm(x, w, eps=EPS):
            xf = x.astype(jnp.float32)
            var = jnp.mean(xf * xf, axis=-1, keepdims=True)
            return (xf * jax.lax.rsqrt(var + eps)).astype(x.dtype) * w
        b, s, _ = hidden_states.shape
        se = encoder_hidden_states.shape[1]
        q = (hidden_states @ Wq + bq).reshape(b, s, NH, HD).transpose(0, 2, 1, 3)
        k = (encoder_hidden_states @ Wk + bk).reshape(b, se, NKV, HD).transpose(0, 2, 1, 3)
        v = (encoder_hidden_states @ Wv + bv).reshape(b, se, NKV, HD).transpose(0, 2, 1, 3)
        k = jnp.repeat(k, GROUPS, axis=1)
        v = jnp.repeat(v, GROUPS, axis=1)
        q = _rmsnorm(q, qn_w)
        k = _rmsnorm(k, kn_w)
        scale = 1.0 / np.sqrt(HD).astype(np.float32)
        scores = jnp.einsum('bhsd,bhed->bhse', q, k) * scale
        scores = scores + attention_mask[:, None, :, :]
        probs = jax.nn.softmax(scores.astype(jnp.float32), axis=-1).astype(q.dtype)
        out = jnp.einsum('bhse,bhed->bhsd', probs, v)
        out = out.transpose(0, 2, 1, 3).reshape(b, s, NH * HD)
        return out @ Wo

    def _L0_ffn_ref(x, w_router, wg, wu, wd, sg, su, sd):
        import jax, jax.numpy as jnp
        import numpy as np
        E, TOPK, H, I, NSH = (8, 2, 256, 640, 2)
        B, S = (2, 128)
        b, s, h = x.shape
        xt = x.reshape(-1, h)
        T = xt.shape[0]
        logits = jnp.einsum('th,eh->te', xt.astype(jnp.float32), w_router.astype(jnp.float32))
        scores = jax.nn.sigmoid(logits)
        topk_w, topk_i = jax.lax.top_k(scores, TOPK)
        topk_w = topk_w / jnp.sum(topk_w, axis=-1, keepdims=True)
        comb = jnp.zeros((T, E), dtype=xt.dtype)
        comb = comb.at[jnp.arange(T)[:, None], topk_i].add(topk_w.astype(xt.dtype))
        gate = jax.nn.silu(jnp.einsum('th,eih->tei', xt, wg))
        up = jnp.einsum('th,eih->tei', xt, wu)
        expert_out = jnp.einsum('tei,ehi->teh', gate * up, wd)
        out = jnp.einsum('te,teh->th', comb, expert_out)
        sgate = jax.nn.silu(jnp.einsum('th,jih->tji', xt, sg))
        sup = jnp.einsum('th,jih->tji', xt, su)
        out = out + jnp.einsum('tji,jhi->th', sgate * sup, sd)
        return out.reshape(b, s, h)
    x = x + _L0_attn_ref(_layernorm(x, axis=-1), L0_attn_W_in, L0_attn_conv_w, L0_attn_conv_b, L0_attn_dt_bias, L0_attn_A_log, L0_attn_D_param, L0_attn_norm_w, L0_attn_W_out)
    x = x + _L0_xattn_ref(_layernorm(x, axis=-1), ctx_2048, mask_1xSxS2_ff0, L0_xattn_Wq, L0_xattn_bq, L0_xattn_Wk, L0_xattn_bk, L0_xattn_Wv, L0_xattn_bv, L0_xattn_Wo, L0_xattn_qn_w, L0_xattn_kn_w)
    x = x + _L0_ffn_ref(_layernorm(x, axis=-1), L0_ffn_w_router, L0_ffn_wg, L0_ffn_wu, L0_ffn_wd, L0_ffn_sg, L0_ffn_su, L0_ffn_sd)
    return x

_drawn_inputs = setup_inputs


def setup_inputs(seed=0):
    import zlib

    import numpy as np

    out = dict(_drawn_inputs(seed))
    spreads = {'L0_attn_D_param': (1.0, 0.2),
     'L0_attn_norm_w': (1.0, 0.2),
     'L0_xattn_qn_w': (1.0, 0.6),
     'L0_xattn_kn_w': (1.0, 0.6)}
    factors = {'L0_attn_dt_bias': 8.0,
     'L0_attn_A_log': 8.0,
     'L0_xattn_bq': 8.0,
     'L0_xattn_bk': 8.0,
     'L0_xattn_bv': 5.311,
     'L0_ffn_w_router': 5.587,
     'L0_ffn_wg': 4.897,
     'L0_ffn_wu': 4.845,
     'L0_ffn_wd': 4.842}
    for name, (base, spread) in spreads.items():
        noise = np.random.default_rng([zlib.crc32(name.encode()), seed]).standard_normal(out[name].shape)
        drawn = base * np.exp(spread * noise) if base else spread * noise
        out[name] = jnp.asarray(drawn.astype(out[name].dtype))
    for name, factor in factors.items():
        out[name] = (out[name] * factor).astype(out[name].dtype)
    return out
```

```python
from contextlib import ExitStack

import concourse.bass as bass
from concourse import mybir

F32 = mybir.dt.float32
F32R = mybir.dt.float32r
ALU = mybir.AluOpType
ACT = mybir.ActivationFunctionType
AX_X = mybir.AxisListType.X

P = 128
HID = 256
KK = HID // P
TOK = 8 * 256
NT = TOK // P
TG = 512
NG = TOK // TG
TPG = TG // P


def wait_apart(eng, signal, value, passed):
    eng.wait_ge(signal, value)
    eng.sem_inc(passed, 1)


def layernorm_stats_steps(dve, st, mv, x_of, tiles, ln_stats, ln_aggr, stats_before):
    for n, t in enumerate(tiles):
        dve.bn_stats(st[:, n, :], x_of(t)).then_inc(ln_stats, 1)
    dve.wait_ge(ln_stats, stats_before + len(tiles))
    for n, t in enumerate(tiles):
        last = dve.bn_aggr(mv[:, n, :], st[:, n, :])
    last.then_inc(ln_aggr, 1)


def mamba_phase(nc, xres, ident, x, w_xz, w_bc, w_dt, conv_w, conv_b, dt_bias, a_log, d_param, norm_w, w_out):
    NCT = w_xz.shape[0]
    HD = 64
    HPT = P // HD
    NH = NCT * HPT
    CB = 2
    SEQ = 256
    BG = TG // SEQ
    NB = TOK // SEQ
    TAPS = conv_w.shape[-1]
    EPS = 1e-5
    SERIES = 8
    BASE = 2

    with ExitStack() as ctx:
        def sb(name, shape, dt=F32):
            return ctx.enter_context(nc.sbuf_tensor("m_" + name, shape, dt))

        def sem(name):
            return ctx.enter_context(nc.semaphore("m_" + name))

        passed = sem("passed")

        wbc = sb("wbc", [P, KK, CB * P])
        wdt = sb("wdt", [P, KK, NH])
        cw = sb("cw", [P, NCT + CB, TAPS])
        cb = sb("cb", [P, NCT + CB])
        dtb = sb("dtb", [P, NH])
        neg_a = sb("neg_a", [P, NH])
        d_ch = sb("d_ch", [P, NCT])
        nw = sb("nw", [P, NCT])
        neg_half = sb("neg_half", [P, NT])
        ones = sb("ones", [P, 1])
        upto = sb("upto", [P, P])
        after = sb("after", [P, P])
        st = sb("st", [P, NT, 6])
        mv = sb("mv", [P, NT, 2])
        rstd = sb("rstd", [P, NT])
        xn = sb("xn", [P, 2, HID])
        xT = sb("xT", [P, KK, TOK])
        bcT = sb("bcT", [P, CB, TOK])
        cb_in = sb("cb_in", [P, NT, P])
        cb_over = sb("cb_over", [P, NB, P])
        dt = sb("dt", [P, NT, NH])
        t_u = sb("t_u", [P, NT, NH])
        t_z = sb("t_z", [P, NT, NH])
        t_z2 = sb("t_z2", [P, NT, NH])
        a_cum = sb("a_cum", [P, NT, NH])
        dt_end = sb("dt_end", [P, NB, NH])
        decay_in = sb("decay_in", [P, NB, NH])
        aT = sb("aT", [NH, TOK])
        wxz = sb("wxz", [P, 2, 2, KK, P])
        wo = sb("wo", [P, 2, HID])
        won = sb("won", [P, 2, HID])
        xc = sb("xc", [P, TG])
        th = sb("th", [P, TG])
        xs = sb("xs", [P, 2, TG])
        thz = sb("thz", [P, TG])
        zs = sb("zs", [P, 2, TG])
        a_row = sb("a_row", [1, 2, HPT * TG])
        a_all = sb("a_all", [P, 2, HPT, TG])
        seg = sb("seg", [P, 2, TPG, HPT, P])
        mat = sb("mat", [P, 2, TPG, HPT, P])
        over_s = sb("over_s", [P, BG, P])
        xdt = sb("xdt", [P, TPG, P])
        xend = sb("xend", [P, BG, P])
        y_over = sb("y_over", [P, BG, P])
        y = sb("y", [P, BG, 2, P])
        gy = sb("gy", [P, TG])
        gT = sb("gT", [P, 2, TG])
        g_sq = sb("g_sq", [P, 2, TG])
        g_sum = sb("g_sum", [P, TG])
        r_out = sb("r_out", [P, TPG])

        def pb(name, banks=1):
            return ctx.enter_context(nc.psum_tensor("m_" + name, [P, banks * TG], F32))

        ps_x, ps_z, ps_t, ps_y, ps_o, ps_yT = (pb(n) for n in ("ps_x", "ps_z", "ps_t", "ps_y", "ps_o", "ps_yT"))
        ps_out = pb("ps_out", 2)

        names = """x_loaded small_loaded consts_done ln_stats ln_aggr ln_veps
            ln_rstd normed xT_ready xT_done dt_ready dt_step dt_exp bc_ready bc_scaled bc_conv bc_tanh bc_done
            cb_ready cb_done cum_ready cum_done end_ready end_exp dt_all aT_ready aT_done aT_copied a_stored halved
            x_ready z_ready x_scaled conv_step x_tanh x_silu z_tanh z_silu t_ready xdt_done xend_done
            a_spread seg_done exp_done mat_done y_ready over_ready y_even_done over_done y_odd_done
            yT_ready gy_done g_done g_squared g_summed won_done out_ready over_copied out_zeroed
            sum_ready sum_mean r_veps r_done x_added""".split()
        S = {n: sem(n) for n in names}
        (x_loaded, small_loaded, consts_done, ln_stats, ln_aggr, ln_veps,
         ln_rstd, normed, xT_ready, xT_done, dt_ready, dt_step, dt_exp, bc_ready, bc_scaled, bc_conv, bc_tanh,
         bc_done, cb_ready, cb_done, cum_ready, cum_done, end_ready, end_exp, dt_all, aT_ready, aT_done,
         aT_copied, a_stored, halved, x_ready, z_ready, x_scaled, conv_step, x_tanh, x_silu, z_tanh, z_silu, t_ready, xdt_done,
         xend_done, a_spread, seg_done, exp_done, mat_done, y_ready, over_ready, y_even_done, over_done,
         y_odd_done, yT_ready, gy_done, g_done, g_squared, g_summed, won_done, out_ready, over_copied,
         out_zeroed, sum_ready, sum_mean, r_veps, r_done, x_added) = (S[n] for n in names)

        wxz_loaded, wo_loaded, row_loaded = ([sem(f"{n}{u}") for u in range(2)]
                                             for n in ("wxz_loaded", "wo_loaded", "row_loaded"))

        def loads(n, u):
            return (n - u) * 8 + 16

        a_dram = nc.dram_tensor("a_by_head", [NG, NH, TG], F32, kind="Internal").ap()
        SMALL = 7 + HPT
        CONV = TAPS - 1

        def batches(ap):
            return ap.rearrange("p (b t) -> p b t", b=BG)

        def steps(eng, do, before=None, after_=None):
            with eng.Fori(0, NG) as g:
                if before:
                    before(g)
                do(g, g * NCT, 0, 0, True, False)
                with eng.Fori(0, NCT // 2 - 1) as j:
                    for u in (1, 2):
                        do(g, g * NCT + j * 2 + u, u % 2, j * 2 + u, False, False)
                do(g, g * NCT + NCT - 1, 1, NCT - 1, False, True)
                if after_:
                    after_(g)

        block = ctx.enter_context(nc.Block())

        @block.sync
        def _(sp):
            x_t = x.rearrange("b (n p) c -> p (b n) c", p=P)
            for g in range(NG):
                ts = slice(g * TPG, (g + 1) * TPG)
                sp.dma_start(xres[:, ts, :], x_t[:, ts, :]).then_inc(x_loaded, 16)
            d_by_head = d_param
            small = [(wbc[:], w_bc), (wdt[:], w_dt), (cw[:], conv_w), (cb[:], conv_b),
                     (dtb[:], dt_bias.partition_broadcast(P)), (neg_a[:], a_log.partition_broadcast(P)),
                     (nw[:], norm_w)]
            small += [(d_ch[i * HD:(i + 1) * HD, :], d_by_head[i].partition_broadcast(HD)) for i in range(HPT)]
            for dst, src in small:
                sp.dma_start(dst, src).then_inc(small_loaded, 16)
            sp.wait_ge(aT_done, 1)
            sp.dma_start(a_dram.rearrange("g h t -> h g t"), aT[:].rearrange("h (g t) -> h g t", g=NG))\
                .then_inc(a_stored, 16)
            sp.wait_ge(a_stored, 16)
            a_by_step = a_dram.rearrange("g (c h) t -> (g c) (h t)", h=HPT).unsqueeze(1)
            with sp.Fori(0, NG) as g:
                with sp.Fori(0, NCT // 2) as j:
                    for u in range(2):
                        n = g * NCT + j * 2 + u
                        sp.wait_ge(z_ready, n + 1)
                        sp.dma_start(wxz[:, u], w_xz[j * 2 + u]).then_inc(wxz_loaded[u], 16)
                        sp.wait_ge(won_done, n + 1)
                        sp.dma_start(wo[:, u, :], w_out[j * 2 + u]).then_inc(wo_loaded[u], 16)
                        sp.wait_ge(a_spread, n + 1)
                        sp.dma_start(a_row[0:1, u, :], a_by_step[n]).then_inc(row_loaded[u], 16)

        @block.gpsimd
        def _(pool):
            for sm in (a_spread, mat_done, g_summed, won_done, r_veps, r_done, over_copied):
                pool.sem_inc(sm, BASE)
            pool.memset(neg_half[:], -0.5).then_inc(consts_done, 1)
            pool.memset(ones[:], 1.0).then_inc(consts_done, 1)
            pool.memset(upto[:], 1.0).then_inc(consts_done, 1)
            pool.memset(after[:], 1.0).then_inc(consts_done, 1)
            pool.wait_ge(consts_done, 4)
            pool.affine_select(out=upto[:], in_=upto[:], compare_op=ALU.is_ge, fill=0.0, base=0,
                               pattern=[[1, P]], channel_multiplier=-1).then_inc(consts_done, 1)
            pool.affine_select(out=after[:], in_=after[:], compare_op=ALU.is_gt, fill=0.0, base=0,
                               pattern=[[-1, P]], channel_multiplier=1).then_inc(consts_done, 1)
            pool.wait_ge(ln_aggr, 1)
            pool.tensor_scalar(rstd[:], mv[:, :, 1], EPS, 0.0, ALU.add, ALU.add).then_inc(ln_veps, 1)
            pool.wait_ge(ln_veps, 1)
            pool.tensor_tensor(rstd[:], rstd[:], neg_half[:], ALU.pow).then_inc(ln_rstd, 1)

            def early(g, n, u, c):
                pool.wait_ge(row_loaded[u], loads(n, u))
                wait_apart(pool, seg_done, BASE + n - 1, passed)
                pool.partition_broadcast(a_all[:, u].rearrange("p h t -> p (h t)"), a_row[0:1, u, :])\
                    .then_inc(a_spread, 1)
                pool.wait_ge(wo_loaded[u], loads(n, u))
                wait_apart(pool, out_ready, BASE + n - 1, passed)
                pool.tensor_tensor(won[:, u, :], wo[:, u, :],
                                   nw[:, bass.ds(c, 1)].broadcast_to([P, HID]), ALU.mult).then_inc(won_done, 1)
                pool.wait_ge(exp_done, BASE + n + 1)
                wait_apart(pool, y_ready, BASE + n - 1, passed)
                pool.tensor_tensor(mat[:, u], seg[:, u],
                                   cb_in[:, bass.ds(g * TPG, TPG), :].unsqueeze(2)
                                   .broadcast_to([P, TPG, HPT, P]), ALU.mult).then_inc(mat_done, 1)

            def late(n, u, first):
                wait_apart(pool, g_squared, BASE + n + 1, passed)
                if first:
                    pool.tensor_copy(g_sum[:], g_sq[:, u, :]).then_inc(g_summed, 1)
                else:
                    wait_apart(pool, g_summed, BASE + n, passed)
                    pool.tensor_tensor(g_sum[:], g_sum[:], g_sq[:, u, :], ALU.add).then_inc(g_summed, 1)

            def before(g):
                wait_apart(pool, over_ready, BASE + g * NCT, passed)
                pool.tensor_copy(over_s[:], cb_over[:, bass.ds(g * BG, BG), :]).then_inc(over_copied, 1)
                early(g, g * NCT, 0, 0)

            def step(g, n, u, c, first, last):
                if not last:
                    early(g, n + 1, 1 - u, c + 1)
                late(n, u, first)

            def end(g):
                pool.wait_ge(sum_mean, g + 1)
                wait_apart(pool, x_added, BASE + g * TPG, passed)
                pool.tensor_scalar(r_out[:], r_out[:], 4 * EPS, 0.0, ALU.add, ALU.add).then_inc(r_veps, 1)
                wait_apart(pool, r_veps, BASE + g + 1, passed)
                pool.tensor_tensor(r_out[:], r_out[:], neg_half[:, 0:TPG], ALU.pow).then_inc(r_done, 1)

            pool.wait_ge(cb_done, NT + NB)
            steps(pool, step, before, end)

        @block.scalar
        def _(act):
            for sm in (x_scaled, x_tanh, z_tanh, exp_done, y_even_done, g_squared):
                act.sem_inc(sm, BASE)
            act.wait_ge(small_loaded, 16 * SMALL)
            act.activation(neg_a[:], neg_a[:], ACT.Exp).then_inc(dt_exp, 1)
            for n in range(NT):
                act.wait_ge(xT_ready, n + 1)
                act.activation(xT[:, :, n * P:(n + 1) * P],
                               (ps_t, ps_y)[n % 2][:, 0:HID].rearrange("p (k t) -> p k t", k=KK),
                               ACT.Copy).then_inc(xT_done, 1)
            act.wait_ge(dt_step, 2)
            act.activation(t_u[:], t_u[:], ACT.Exp).then_inc(dt_exp, 1)
            act.wait_ge(halved, 2)

            def bc_tile(m):
                i = m // NG
                act.wait_ge(bc_ready, m + 1)
                if m >= 1:
                    act.wait_ge(bc_done, m)
                act.activation(xc[:], (ps_x, ps_z)[m % 2][:, :], ACT.Identity, bias=cb[:, NCT + i:NCT + i + 1],
                               scale=cw[:, NCT + i, TAPS - 1:TAPS]).then_inc(bc_scaled, 1)
                act.wait_ge(bc_conv, (m + 1) * CONV)
                act.activation(th[:], xc[:], ACT.Tanh).then_inc(bc_tanh, 1)

            for m in range(CB * NG):
                bc_tile(m)
            act.wait_ge(end_ready, 1)
            act.activation(dt_end[:].rearrange("p b h -> p (b h)"), ps_x[:, :], ACT.Exp).then_inc(end_exp, 1)
            act.wait_ge(cum_done, 1)
            act.activation(decay_in[:], a_cum[:].rearrange("p (b c) h -> p b c h", c=2)[:, :, 1, :],
                           ACT.Exp).then_inc(end_exp, 1)
            for n in range(NG):
                act.wait_ge(aT_ready, n + 1)
                act.activation(aT[:, n * TG:(n + 1) * TG], (ps_t, ps_yT)[n % 2][0:NH, :], ACT.Copy)\
                    .then_inc(aT_done if n == NG - 1 else aT_copied, 1)

            def exps(n, u):
                act.wait_ge(seg_done, BASE + n + 1)
                act.activation(seg[:, u], seg[:, u], ACT.Exp).then_inc(exp_done, 1)

            def scale_x(n, c):
                act.wait_ge(x_ready, BASE + n + 1)
                act.wait_ge(x_silu, BASE + n)
                act.activation(xc[:], ps_x[:, :], ACT.Identity, bias=cb[:, bass.ds(c, 1)],
                               scale=cw[:, bass.ds(c, 1), TAPS - 1]).then_inc(x_scaled, 1)

            def tanh_x(n):
                act.wait_ge(conv_step, BASE + (n + 1) * CONV)
                act.activation(th[:], xc[:], ACT.Tanh).then_inc(x_tanh, 1)

            def tanh_z(n):
                act.wait_ge(z_ready, BASE + n + 1)
                act.wait_ge(z_silu, BASE + n)
                act.activation(thz[:], ps_z[:, :], ACT.Tanh, scale=0.5).then_inc(z_tanh, 1)

            def before(g):
                exps(g * NCT, 0)
                scale_x(g * NCT, 0)
                tanh_x(g * NCT)
                tanh_z(g * NCT)

            def step(g, n, u, c, first, last):
                if not last:
                    exps(n + 1, 1 - u)
                    scale_x(n + 1, c + 1)
                act.wait_ge(y_ready, BASE + n + 1)
                act.wait_ge(yT_ready, BASE + n)
                act.activation(y[:, :, 0, :], ps_y[:, 0:BG * P].rearrange("p (b t) -> p b t", b=BG),
                               ACT.Copy).then_inc(y_even_done, 1)
                if not last:
                    tanh_x(n + 1)
                act.wait_ge(g_done, BASE + n + 1)
                act.wait_ge(g_summed, BASE + n - 1)
                act.activation(g_sq[:, u, :], gT[:, u, :], ACT.Square).then_inc(g_squared, 1)
                if not last:
                    tanh_z(n + 1)

            steps(act, step, before)

        @block.vector
        def _(dve):
            for sm in (conv_step, x_silu, z_silu, xdt_done, xend_done, seg_done, over_done, y_odd_done, gy_done,
                       g_done, x_added, out_zeroed):
                dve.sem_inc(sm, BASE)
            dve.wait_ge(x_loaded, 16 * NG)
            layernorm_stats_steps(dve, st, mv, lambda t: xres[:, t, :], range(NT), ln_stats, ln_aggr, 0)
            dve.wait_ge(small_loaded, 16 * SMALL)
            dve.tensor_scalar(cw[:], cw[:], 0.5, None, ALU.mult).then_inc(halved, 1)
            dve.tensor_scalar(cb[:], cb[:], 0.5, None, ALU.mult).then_inc(halved, 1)
            dve.wait_ge(ln_rstd, 1)
            for n in range(NT):
                if n >= 2:
                    dve.wait_ge(xT_ready, n - 1)
                dve.tensor_scalar(xn[:, n % 2, :], xres[:, n, :], mv[:, n, 0:1], rstd[:, n:n + 1],
                                  ALU.subtract, ALU.mult).then_inc(normed, 1)

            count = [0]

            def then(ins):
                count[0] += 1
                ins.then_inc(dt_step, 1)
                dve.wait_ge(dt_step, count[0])

            all_heads = [P, NT, NH]
            dve.wait_ge(dt_ready, 1)
            then(dve.tensor_tensor(dt[:], ps_out[:, :].rearrange("p (t h) -> p t h", t=NT),
                                   dtb[:].unsqueeze(1).broadcast_to(all_heads), ALU.add))
            then(dve.scalar_tensor_tensor(out=t_u[:], in0=dt[:], scalar=-1.0, in1=dt[:],
                                          op0=ALU.mult, op1=ALU.min))
            dve.wait_ge(dt_exp, 2)
            then(dve.tensor_scalar(t_z[:], t_u[:], 2.0, None, ALU.add))
            then(dve.reciprocal(t_z[:], t_z[:]))
            then(dve.tensor_tensor(t_z[:], t_z[:], t_u[:], ALU.mult))
            then(dve.tensor_tensor(t_z2[:], t_z[:], t_z[:], ALU.mult))
            then(dve.tensor_scalar(t_u[:], t_z2[:], 1.0 / (2 * SERIES + 1), None, ALU.mult))
            for k in range(SERIES - 1, 0, -1):
                then(dve.scalar_tensor_tensor(out=t_u[:], in0=t_u[:], scalar=1.0 / (2 * k + 1), in1=t_z2[:],
                                              op0=ALU.add, op1=ALU.mult))
            then(dve.scalar_tensor_tensor(out=t_u[:], in0=t_u[:], scalar=1.0, in1=t_z[:],
                                          op0=ALU.add, op1=ALU.mult))
            then(dve.tensor_scalar(dt[:], dt[:], 0.0, None, ALU.max))
            then(dve.scalar_tensor_tensor(out=dt[:], in0=t_u[:], scalar=2.0, in1=dt[:],
                                          op0=ALU.mult, op1=ALU.add))
            then(dve.tensor_scalar(neg_a[:], neg_a[:], -1.0, None, ALU.mult))
            dve.tensor_tensor(t_z[:], dt[:], neg_a[:].unsqueeze(1).broadcast_to(all_heads), ALU.mult)\
                .then_inc(dt_all, 1)

            def conv(ps, w_of, sm, base):
                for i in range(1, TAPS):
                    dve.scalar_tensor_tensor(
                        out=batches(xc[:])[:, :, i:], in0=batches(ps)[:, :, 0:SEQ - i],
                        scalar=w_of(TAPS - 1 - i), in1=batches(xc[:])[:, :, i:],
                        op0=ALU.mult, op1=ALU.add).then_inc(sm, 1)
                    if i < TAPS - 1:
                        dve.wait_ge(sm, base + i)

            for m in range(CB * NG):
                i, g = m // NG, m % NG
                dve.wait_ge(bc_scaled, m + 1)
                conv((ps_x, ps_z)[m % 2][:, :], lambda k: cw[:, NCT + i, k:k + 1], bc_conv, m * CONV)
                dve.wait_ge(bc_tanh, m + 1)
                dve.scalar_tensor_tensor(out=bcT[:, i, g * TG:(g + 1) * TG], in0=th[:], scalar=1.0, in1=xc[:],
                                         op0=ALU.add, op1=ALU.mult).then_inc(bc_done, 1)
            dve.wait_ge(cum_ready, 1)
            dve.tensor_copy(a_cum[:].rearrange("p t h -> p (t h)"), ps_out[:, :]).then_inc(cum_done, 1)
            dve.wait_ge(end_exp, 1)
            first_chunks = dt[:].rearrange("p (b c) h -> p b c h", c=2)[:, :, 0, :]
            dve.tensor_tensor(dt_end[:], dt_end[:], first_chunks, ALU.mult).then_inc(dt_all, 1)
            for b in range(NT // 4):
                dve.wait_ge(cb_ready, b + 1)
                for i in range(4):
                    dve.tensor_tensor(cb_in[:, b * 4 + i, :], (ps_o, ps_y)[b % 2][:, i * P:(i + 1) * P],
                                      upto[:], ALU.mult).then_inc(cb_done, 1)
            for b in range(NB // 4):
                dve.wait_ge(cb_ready, NT // 4 + b + 1)
                for i in range(4):
                    dve.tensor_copy(cb_over[:, b * 4 + i, :], (ps_o, ps_y)[b % 2][:, i * P:(i + 1) * P])\
                        .then_inc(cb_done, 1)
            dve.wait_ge(aT_done, 1)
            dve.wait_ge(dt_all, 2)

            def seg_of(g, n, u, c):
                dve.wait_ge(a_spread, BASE + n + 1)
                dve.wait_ge(mat_done, BASE + n - 1)
                for q in range(TPG):
                    for h in range(HPT):
                        last = dve.tensor_scalar(
                            seg[:, u, q, h, :], a_all[:, u, h, q * P:(q + 1) * P],
                            a_cum[:, bass.ds(g * TPG + q, 1), bass.ds(c * HPT + h, 1)].rearrange("p a b -> p (a b)"),
                            0.0, ALU.subtract, ALU.min)
                last.then_inc(seg_done, 1)

            def conv_x(n, c):
                dve.wait_ge(x_scaled, BASE + n + 1)
                conv(ps_x[:, :], lambda k: cw[:, bass.ds(c, 1), k], conv_step, BASE + n * CONV)

            def silu_x(n, u):
                dve.wait_ge(x_tanh, BASE + n + 1)
                dve.wait_ge(gy_done, BASE + n - 1)
                dve.scalar_tensor_tensor(out=xs[:, u, :], in0=th[:], scalar=1.0, in1=xc[:],
                                         op0=ALU.add, op1=ALU.mult).then_inc(x_silu, 1)

            def silu_z(n, u):
                dve.wait_ge(z_tanh, BASE + n + 1)
                dve.wait_ge(g_done, BASE + n - 1)
                dve.scalar_tensor_tensor(out=zs[:, u, :], in0=thz[:], scalar=1.0, in1=ps_z[:, :],
                                         op0=ALU.add, op1=ALU.mult).then_inc(z_silu, 1)

            def before(g):
                dve.wait_ge(x_added, BASE + g * TPG)
                dve.memset(ps_out[:, :], 0.0).then_inc(out_zeroed, 1)
                seg_of(g, g * NCT, 0, 0)
                conv_x(g * NCT, 0)
                silu_x(g * NCT, 0)
                silu_z(g * NCT, 0)

            def step(g, n, u, c, first, last):
                dve.wait_ge(t_ready, BASE + n + 1)
                dve.wait_ge(y_ready, BASE + n)
                heads = bass.ds(c * HPT, HPT)
                x_t = ps_t[:, :].rearrange("p (t h d) -> p t h d", t=TPG, h=HPT)
                dve.tensor_tensor(xdt[:].rearrange("p t (h d) -> p t h d", h=HPT), x_t,
                                  dt[:, bass.ds(g * TPG, TPG), heads].unsqueeze(3)
                                  .broadcast_to([P, TPG, HPT, HD]), ALU.mult).then_inc(xdt_done, 1)
                dve.wait_ge(over_ready, BASE + n)
                dve.tensor_tensor(xend[:].rearrange("p b (h d) -> p b h d", h=HPT),
                                  x_t.rearrange("p (b c) h d -> p b c h d", c=2)[:, :, 0],
                                  dt_end[:, bass.ds(g * BG, BG), heads].unsqueeze(3)
                                  .broadcast_to([P, BG, HPT, HD]), ALU.mult).then_inc(xend_done, 1)
                if not last:
                    seg_of(g, n + 1, 1 - u, c + 1)
                    conv_x(n + 1, c + 1)
                dve.wait_ge(over_ready, BASE + n + 1)
                dve.tensor_tensor(y_over[:].rearrange("p b (h d) -> p b h d", h=HPT),
                                  ps_o[:, 0:BG * P].rearrange("p (b h d) -> p b h d", b=BG, h=HPT),
                                  decay_in[:, bass.ds(g * BG, BG), heads].unsqueeze(3)
                                  .broadcast_to([P, BG, HPT, HD]), ALU.mult).then_inc(over_done, 1)
                dve.wait_ge(over_done, BASE + n + 1)
                dve.wait_ge(yT_ready, BASE + n)
                dve.tensor_tensor(y[:, :, 1, :],
                                  ps_o[:, BG * P:].rearrange("p (b t) -> p b t", b=BG),
                                  y_over[:], ALU.add).then_inc(y_odd_done, 1)
                if not last:
                    silu_x(n + 1, 1 - u)
                dve.wait_ge(yT_ready, BASE + n + 1)
                dve.wait_ge(g_done, BASE + n)
                dve.scalar_tensor_tensor(out=gy[:], in0=xs[:, u, :], scalar=d_ch[:, bass.ds(c, 1)],
                                         in1=ps_yT[:, :], op0=ALU.mult, op1=ALU.add).then_inc(gy_done, 1)
                dve.wait_ge(gy_done, BASE + n + 1)
                dve.wait_ge(out_ready, BASE + n - 1)
                dve.wait_ge(g_squared, BASE + n - 1)
                dve.tensor_tensor(gT[:, u, :], gy[:], zs[:, u, :], ALU.mult).then_inc(g_done, 1)
                if not last:
                    silu_z(n + 1, 1 - u)

            def end(g):
                dve.wait_ge(sum_ready, g + 1)
                dve.tensor_scalar(r_out[:], ps_o[:, 0:TPG], 1.0 / (NCT * P), None, ALU.mult)\
                    .then_inc(sum_mean, 1)
                dve.wait_ge(r_done, BASE + g + 1)
                dve.wait_ge(out_ready, BASE + (g + 1) * NCT)
                for q in range(TPG):
                    tile = xres[:, bass.ds(g * TPG + q, 1), :].rearrange("p a c -> p (a c)")
                    dve.scalar_tensor_tensor(out=tile, in0=ps_out[:, q * HID:(q + 1) * HID],
                                             scalar=r_out[:, q:q + 1], in1=tile,
                                             op0=ALU.mult, op1=ALU.add).then_inc(x_added, 1)

            steps(dve, step, before, end)

        @block.tensor
        def _(pe):
            for sm in (x_ready, z_ready, t_ready, y_ready, over_ready, yT_ready, out_ready):
                pe.sem_inc(sm, BASE)
            for n in range(NT):
                pe.wait_ge(normed, n + 1)
                if n >= 2:
                    pe.wait_ge(xT_done, n - 1)
                for k in range(KK):
                    last = pe.transpose((ps_t, ps_y)[n % 2][:, k * P:(k + 1) * P],
                                        xn[:, n % 2, k * P:(k + 1) * P], ident)
                last.then_inc(xT_ready, 1)
            pe.wait_ge(xT_done, NT)
            pe.wait_ge(small_loaded, 16 * SMALL)
            for n in range(NT):
                for k in range(KK):
                    last = pe.matmul(ps_out[:, n * NH:(n + 1) * NH], xT[:, k, n * P:(n + 1) * P], wdt[:, k, :],
                                     start=k == 0, stop=k == KK - 1)
            last.then_inc(dt_ready, 1)
            for m in range(CB * NG):
                i, g = m // NG, m % NG
                if m >= 2:
                    pe.wait_ge(bc_done, m - 1)
                for k in range(KK):
                    last = pe.matmul((ps_x, ps_z)[m % 2][:, :], wbc[:, k, i * P:(i + 1) * P],
                                     xT[:, k, g * TG:(g + 1) * TG], start=k == 0, stop=k == KK - 1)
                last.then_inc(bc_ready, 1)
            pe.wait_ge(dt_all, 1)
            pe.wait_ge(consts_done, 6)
            for n in range(NT):
                last = pe.matmul(ps_out[:, n * NH:(n + 1) * NH], upto[:], t_z[:, n, :], start=True, stop=True)
            last.then_inc(cum_ready, 1)
            pe.wait_ge(bc_done, CB * NG)
            for b in range(NB):
                last = pe.matmul(ps_x[:, b * NH:(b + 1) * NH], after[:], t_z[:, 2 * b, :], start=True, stop=True)
            last.then_inc(end_ready, 1)
            for b in range(NT // 4):
                if b >= 2:
                    pe.wait_ge(cb_done, (b - 1) * 4)
                for i in range(4):
                    t = slice((b * 4 + i) * P, (b * 4 + i + 1) * P)
                    last = pe.matmul((ps_o, ps_y)[b % 2][:, i * P:(i + 1) * P], bcT[:, 0, t], bcT[:, 1, t],
                                     start=True, stop=True)
                last.then_inc(cb_ready, 1)
            for b in range(NB // 4):
                pe.wait_ge(cb_done, NT + (b - 1) * 4)
                for i in range(4):
                    t = (b * 4 + i) * 2
                    last = pe.matmul((ps_o, ps_y)[b % 2][:, i * P:(i + 1) * P],
                                     bcT[:, 0, t * P:(t + 1) * P], bcT[:, 1, (t + 1) * P:(t + 2) * P],
                                     start=True, stop=True)
                last.then_inc(cb_ready, 1)
            pe.wait_ge(cum_done, 1)
            for b in range(NG):
                if b >= 2:
                    pe.wait_ge(aT_copied, b - 1)
                for i in range(TPG):
                    last = pe.transpose((ps_t, ps_yT)[b % 2][0:NH, i * P:(i + 1) * P],
                                        a_cum[:, b * TPG + i, :], ident)
                last.then_inc(aT_ready, 1)
            pe.wait_ge(cb_done, NT + NB)
            pe.wait_ge(aT_done, 1)
            pe.wait_ge(end_exp, 1)

            def project(g, n, u, which, ps, ready):
                for k in range(KK):
                    last = pe.matmul(ps[:, :], wxz[:, u, which, k, :], xT[:, k, bass.ds(g * TG, TG)],
                                     start=k == 0, stop=k == KK - 1)
                last.then_inc(ready, 1)

            def x_proj(g, n, u):
                pe.wait_ge(wxz_loaded[u], loads(n, u))
                pe.wait_ge(conv_step, BASE + n * CONV)
                project(g, n, u, 0, ps_x, x_ready)

            def z_proj(g, n, u):
                pe.wait_ge(z_silu, BASE + n)
                project(g, n, u, 1, ps_z, z_ready)

            def out_proj(n, u):
                pe.wait_ge(g_done, BASE + n + 1)
                pe.wait_ge(won_done, BASE + n + 1)
                for q in range(TPG):
                    last = pe.matmul(ps_out[:, q * HID:(q + 1) * HID], gT[:, u, q * P:(q + 1) * P],
                                     won[:, u, :], start=False, stop=True, skip_group_check=True)
                last.then_inc(out_ready, 1)

            def before(g):
                pe.wait_ge(over_copied, BASE + g + 1)
                x_proj(g, g * NCT, 0)
                z_proj(g, g * NCT, 0)
                pe.wait_ge(out_zeroed, BASE + g + 1)

            def step(g, n, u, c, first, last):
                pe.wait_ge(x_silu, BASE + n + 1)
                pe.wait_ge(xend_done, BASE + n)
                for q in range(TPG):
                    ins = pe.transpose(ps_t[:, q * P:(q + 1) * P], xs[:, u, q * P:(q + 1) * P], ident)
                ins.then_inc(t_ready, 1)
                if not last:
                    x_proj(g, n + 1, 1 - u)
                pe.wait_ge(mat_done, BASE + n + 1)
                pe.wait_ge(xdt_done, BASE + n + 1)
                pe.wait_ge(y_even_done, BASE + n)
                pe.wait_ge(y_odd_done, BASE + n)
                for q in range(TPG):
                    for h in range(HPT):
                        ps, at = (ps_y, ps_o)[q % 2], (q % 2 * BG + q // 2) * P + h * HD
                        ins = pe.matmul(ps[:, at:at + HD], mat[:, u, q, h, :], xdt[:, q, h * HD:(h + 1) * HD],
                                        start=True, stop=True)
                ins.then_inc(y_ready, 1)
                pe.wait_ge(xend_done, BASE + n + 1)
                pe.wait_ge(over_done, BASE + n)
                for b in range(BG):
                    ins = pe.matmul(ps_o[:, b * P:(b + 1) * P], over_s[:, b, :], xend[:, b, :],
                                    start=True, stop=True)
                ins.then_inc(over_ready, 1)
                if not first:
                    out_proj(n - 1, 1 - u)
                pe.wait_ge(y_odd_done, BASE + n + 1)
                pe.wait_ge(y_even_done, BASE + n + 1)
                pe.wait_ge(gy_done, BASE + n)
                for q in range(TPG):
                    ins = pe.transpose(ps_yT[:, q * P:(q + 1) * P], y[:, q // 2, q % 2, :], ident)
                ins.then_inc(yT_ready, 1)
                if not last:
                    z_proj(g, n + 1, 1 - u)

            def end(g):
                out_proj(g * NCT + NCT - 1, 1)
                pe.wait_ge(g_summed, BASE + (g + 1) * NCT)
                for q in range(TPG):
                    ins = pe.matmul(ps_o[:, q:q + 1], g_sum[:, q * P:(q + 1) * P], ones[:], start=True, stop=True)
                ins.then_inc(sum_ready, 1)

            steps(pe, step, before, end)


def cross_attention_phase(nc, xres, ident, ctx_T, mask, wq, bq, wk, bk, wv, bv, wo, qn, kn):
    D = P
    NH = wq.shape[-1] // D
    NKV = wk.shape[-1] // D
    PER = NH // NKV
    SE = mask.shape[-1]
    BG = ctx_T.shape[3]
    HB = 4
    NB = NH // HB
    EPS_LN, EPS_RMS = 1e-5, 1e-6
    BASE = 1

    with ExitStack() as ctx:
        def sb(name, shape, dt=F32):
            return ctx.enter_context(nc.sbuf_tensor("a_" + name, shape, dt))

        def sem(name):
            return ctx.enter_context(nc.semaphore("a_" + name))

        passed, passed_dve, passed_sp = (sem(n) for n in ("passed", "passed_dve", "passed_sp"))

        st = sb("st", [P, TPG, 6])
        mv = sb("mv", [P, TPG, 2])
        rstd = sb("rstd", [P, TPG])
        neg_half = sb("neg_half", [P, TPG])
        ones = sb("ones", [P, P])
        eps_rms = sb("eps_rms", [P, 1])
        xn = sb("xn", [P, 2, HID])
        xT_hi = sb("xT_hi", [P, KK, TG], F32R)
        xT_lo = sb("xT_lo", [P, KK, TG], F32R)
        raw = sb("raw", [P, KK, NH * D])
        wq_hi = sb("wq_hi", [P, KK, NH * D], F32R)
        wq_lo = sb("wq_lo", [P, KK, NH * D], F32R)
        wo_hi = sb("wo_hi", [P, NH, HID], F32R)
        wo_lo = sb("wo_lo", [P, NH, HID], F32R)
        wk_sb = sb("wk", [P, KK, NKV * D])
        wv_sb = sb("wv", [P, KK, NKV * D])
        bq_sb = sb("bq", [P, NH])
        bk_sb = sb("bk", [P, NKV])
        bv_sb = sb("bv", [P, NKV * D])
        qn_sb = sb("qn", [P, 1])
        kn_sb = sb("kn", [P, 1])
        qkn = sb("qkn", [P, 1])
        mask_sb = sb("mask", [P, 2, SE])
        cT = sb("cT", [P, KK, BG, 2, SE])
        kT = sb("kT", [P, NKV, BG * SE])
        k_sq = sb("k_sq", [P, NKV, BG * SE])
        k_var = sb("k_var", [P, NKV, BG * SE])
        v = sb("v", [P, BG, NKV * D])
        qT = sb("qT", [P, NH, TG])
        q_sq = sb("q_sq", [P, 2, TG])
        q_var = sb("q_var", [P, TPG, NH])
        s = sb("s", [P, 2, NH, SE])
        s_max = sb("s_max", [P, NH])
        s_sum = sb("s_sum", [P, NH])
        pT = sb("pT", [P, NH // 2, P])
        oT_hi = sb("oT_hi", [P, NH, P], F32R)
        oT_lo = sb("oT_lo", [P, NH, P], F32R)

        def pb(name, banks=1):
            return ctx.enter_context(nc.psum_tensor("a_" + name, [P, banks * TG], F32))

        ps_q = pb("ps_q", 2)
        ps_s = pb("ps_s", 2)
        ps_o = pb("ps_o", 2)
        ps_ss = pb("ps_ss")
        ps_out = pb("ps_out")
        bank = lambda t, n: t[:, n * TG:(n + 1) * TG]

        wq_loaded, wo_loaded = sem("wq_loaded"), sem("wo_loaded")
        small_loaded, ctx_loaded = sem("small_loaded"), sem("ctx_loaded")
        w_copied, w_split = sem("w_copied"), sem("w_split")
        consts_done = sem("consts_done")
        qkn_done = sem("qkn_done")
        ln_stats, ln_aggr, ln_veps, ln_rstd = (sem(n) for n in ("ln_stats", "ln_aggr", "ln_veps", "ln_rstd"))
        normed, xT_ready, xT_hi_done, xT_lo_done = (
            sem(n) for n in ("normed", "xT_ready", "xT_hi_done", "xT_lo_done"))
        k_ready, k_biased, k_squared, k_summed = (
            sem(n) for n in ("k_ready", "k_biased", "k_squared", "k_summed"))
        k_root_done, k_rstd_done, k_done = (sem(n) for n in ("k_root_done", "k_rstd_done", "k_done"))
        v_ready, v_done = sem("v_ready"), sem("v_done")
        q_ready, q_done, q_squared, q_summed = (
            sem(n) for n in ("q_ready", "q_done", "q_squared", "q_summed"))
        q_root_done, q_rstd_done = sem("q_root_done"), sem("q_rstd_done")
        scores_ready, soft_step, exp_done = sem("scores_ready"), sem("soft_step"), sem("exp_done")
        pT_ready, pT_done = sem("pT_ready"), sem("pT_done")
        o_ready, o_hi_done, o_lo_done = sem("o_ready"), sem("o_hi_done"), sem("o_lo_done")
        out_ready, out_added = sem("out_ready"), sem("out_added")

        SOFT_A, SOFT = 4, 7
        groups = range(TPG)

        def heads_of(b):
            return range(b // 2 * 2 * HB + b % 2, (b // 2 + 1) * 2 * HB, 2)

        block = ctx.enter_context(nc.Block())

        @block.sync
        def _(sp):
            sp.dma_start(raw[:], wq).then_inc(wq_loaded, 16)
            small = ((wk_sb[:], wk), (wv_sb[:], wv), (bq_sb[:], bq), (bk_sb[:], bk),
                     (bv_sb[:], bv.partition_broadcast(P)), (qn_sb[:], qn), (kn_sb[:], kn),
                     (mask_sb[:], mask))
            for dst, src in small:
                sp.dma_start(dst, src).then_inc(small_loaded, 16)
            sp.wait_ge(w_split, 1)
            sp.dma_start(raw[:].rearrange("p k n -> p (k n)"), wo).then_inc(wo_loaded, 16)
            sp.sem_inc(ctx_loaded, BASE)
            with sp.Fori(0, NG) as g:
                wait_apart(sp, v_ready, BASE + g * BG, passed_sp)
                wait_apart(sp, k_ready, BASE + g, passed_sp)
                for twin in range(2):
                    for k in range(KK):
                        sp.dma_start(cT[:, k, :, twin, :], ctx_T[g, :, k, :, :]).then_inc(ctx_loaded, 16)

        @block.gpsimd
        def _(pool):
            pool.memset(neg_half[:], -0.5).then_inc(consts_done, 1)
            pool.memset(ones[:], 1.0).then_inc(consts_done, 1)
            pool.memset(eps_rms[:], EPS_RMS).then_inc(consts_done, 1)
            pool.wait_ge(wq_loaded, 16)
            pool.tensor_copy(wq_hi[:], raw[:]).then_inc(w_copied, 1)
            pool.wait_ge(w_copied, 1)
            pool.tensor_tensor(wq_lo[:], raw[:], wq_hi[:].bitcast(F32), ALU.subtract).then_inc(w_split, 1)

            pool.sem_inc(ln_veps, BASE)
            pool.sem_inc(ln_rstd, BASE)
            with pool.Fori(0, NG) as g:
                wait_apart(pool, ln_aggr, BASE + g + 1, passed)
                pool.tensor_scalar(rstd[:], mv[:, :, 1], EPS_LN, 0.0, ALU.add, ALU.add)\
                    .then_inc(ln_veps, 1)
                wait_apart(pool, ln_veps, BASE + g + 1, passed)
                pool.tensor_tensor(rstd[:], rstd[:], neg_half[:], ALU.pow).then_inc(ln_rstd, 1)

        @block.scalar
        def _(act):
            act.sem_inc(q_done, BASE)
            act.sem_inc(k_biased, BASE)
            act.sem_inc(pT_done, BASE)
            act.sem_inc(o_hi_done, BASE)
            act.wait_ge(small_loaded, 16 * 8)
            act.wait_ge(consts_done, 3)
            with act.Fori(0, NG) as g:
                for q in groups:
                    act.wait_ge(xT_ready, BASE + g * TPG + q + 1)
                    act.activation(xT_hi[:, :, q * P:(q + 1) * P],
                                   bank(ps_q, q % 2)[:, 0:HID].rearrange("p (k t) -> p k t", k=KK),
                                   ACT.Copy).then_inc(xT_hi_done, 1)
                act.wait_ge(k_ready, BASE + g + 1)
                for kv in range(NKV):
                    cols = slice(kv * BG * SE, (kv + 1) * BG * SE)
                    act.activation(kT[:, kv, :], ps_out[:, cols], ACT.Identity,
                                   bias=bk_sb[:, kv:kv + 1]).then_inc(k_biased, 1)
                for h in range(NH):
                    act.wait_ge(q_ready, BASE + g * NH + h + 1)
                    act.activation(qT[:, h, :], bank(ps_q, h % 2), ACT.Identity,
                                   bias=bq_sb[:, h:h + 1]).then_inc(q_done, 1)
                    if h == 1:
                        act.wait_ge(k_summed, g + 1)
                        act.activation(k_var[:].rearrange("p g t -> p (g t)"), bank(ps_o, 0), ACT.Sqrt,
                                       bias=eps_rms[:, 0:1], scale=1.0 / D).then_inc(k_root_done, 1)
                act.wait_ge(q_summed, (g + 1) * NH)
                act.activation(q_var[:].rearrange("p t h -> p (t h)"), ps_ss[:, 0:TPG * NH], ACT.Sqrt,
                               bias=eps_rms[:, 0:1], scale=1.0 / D).then_inc(q_root_done, 1)

                def exp(q):
                    act.wait_ge(soft_step, BASE + (g * TPG + q) * SOFT + SOFT_A)
                    act.activation(s[:, q % 2], s[:, q % 2], ACT.Exp).then_inc(exp_done, 1)

                exp(0)
                for q in groups:
                    act.wait_ge(pT_ready, BASE + g * TPG + q + 1)
                    act.wait_ge(o_ready, BASE + (g * TPG + q) * NB)
                    act.activation(pT[:].rearrange("p n t -> p (n t)"), ps_q[:, :], ACT.Copy)\
                        .then_inc(pT_done, 1)
                    for b in range(NB):
                        act.wait_ge(o_ready, BASE + (g * TPG + q) * NB + b + 1)
                        act.wait_ge(out_ready, BASE + g * TPG + q)
                        act.activation(oT_hi[:, b * HB:(b + 1) * HB, :].rearrange("p h t -> p (h t)"),
                                       bank(ps_o, b % 2), ACT.Copy).then_inc(o_hi_done, 1)
                        if b == 0 and q + 1 < TPG:
                            exp(q + 1)

        @block.vector
        def _(dve):
            for sm in (ln_stats, ln_aggr, xT_lo_done, normed, q_squared, soft_step, o_lo_done, v_done, k_squared,
                       out_added):
                dve.sem_inc(sm, BASE)
            dve.wait_ge(small_loaded, 16 * 8)
            dve.scalar_tensor_tensor(out=qkn[:], in0=qn_sb[:], scalar=float(D) ** -0.5, in1=kn_sb[:],
                                     op0=ALU.mult, op1=ALU.mult).then_inc(qkn_done, 1)
            dve.wait_ge(consts_done, 2)
            dve.wait_ge(wo_loaded, 16)
            wo_raw = raw[:].rearrange("p k n -> p (k n)").rearrange("p (h n) -> p h n", h=NH)
            dve.tensor_copy(wo_hi[:], wo_raw).then_inc(w_copied, 1)
            dve.wait_ge(w_copied, 2)
            dve.tensor_tensor(wo_lo[:], wo_raw, wo_hi[:].bitcast(F32), ALU.subtract).then_inc(w_split, 1)

            with dve.Fori(0, NG) as g:
                dve.wait_ge(ln_aggr, BASE + g)
                for q in groups:
                    dve.bn_stats(st[:, q, :], xres[:, bass.ds(g * TPG + q, 1), :].rearrange("p a c -> p (a c)"))\
                        .then_inc(ln_stats, 1)
                wait_apart(dve, ln_stats, BASE + g * TPG + TPG, passed_dve)
                for q in groups:
                    last = dve.bn_aggr(mv[:, q, :], st[:, q, :])
                last.then_inc(ln_aggr, 1)
                dve.wait_ge(ln_rstd, BASE + g + 1)

                def xT_low(q):
                    dve.wait_ge(xT_hi_done, g * TPG + q + 1)
                    ts = slice(q * P, (q + 1) * P)
                    dve.tensor_tensor(xT_lo[:, :, ts],
                                      bank(ps_q, q % 2)[:, 0:HID].rearrange("p (k t) -> p k t", k=KK),
                                      xT_hi[:, :, ts].bitcast(F32), ALU.subtract).then_inc(xT_lo_done, 1)

                for q in groups:
                    if q >= 2:
                        dve.wait_ge(xT_ready, BASE + g * TPG + q - 1)
                    dve.tensor_scalar(xn[:, q % 2, :],
                                      xres[:, bass.ds(g * TPG + q, 1), :].rearrange("p a c -> p (a c)"),
                                      mv[:, q, 0:1], rstd[:, q:q + 1],
                                      ALU.subtract, ALU.mult).then_inc(normed, 1)
                    if q > 0:
                        xT_low(q - 1)
                xT_low(TPG - 1)

                dve.wait_ge(k_biased, BASE + (g + 1) * NKV)
                dve.tensor_tensor(k_sq[:], kT[:], kT[:], ALU.mult).then_inc(k_squared, 1)
                for hb in range(BG):
                    dve.wait_ge(v_ready, BASE + g * BG + hb + 1)
                    dve.tensor_tensor(v[:, hb, :], bank(ps_s, hb), bv_sb[:], ALU.add).then_inc(v_done, 1)
                for h in range(NH):
                    dve.wait_ge(q_done, BASE + g * NH + h + 1)
                    if h >= 2:
                        dve.wait_ge(q_summed, g * NH + h - 1)
                    dve.tensor_tensor(q_sq[:, h % 2, :], qT[:, h, :], qT[:, h, :], ALU.mult)\
                        .then_inc(q_squared, 1)
                    if h == 3:
                        dve.wait_ge(k_root_done, g + 1)
                        dve.reciprocal(k_var[:], k_var[:]).then_inc(k_rstd_done, 1)
                        dve.wait_ge(k_rstd_done, g + 1)
                        dve.scalar_tensor_tensor(out=kT[:], in0=kT[:], scalar=qkn[:, 0:1], in1=k_var[:],
                                                 op0=ALU.mult, op1=ALU.mult).then_inc(k_done, 1)
                dve.wait_ge(q_root_done, g + 1)
                dve.reciprocal(q_var[:], q_var[:]).then_inc(q_rstd_done, 1)
                dve.wait_ge(q_rstd_done, g + 1)

                full = [P, NH, SE]

                def then(ins, q, n):
                    ins.then_inc(soft_step, 1)
                    dve.wait_ge(soft_step, BASE + (g * TPG + q) * SOFT + n)

                def softmax_a(q):
                    sc = s[:, q % 2]
                    dve.wait_ge(scores_ready, BASE + g * TPG + q + 1)
                    then(dve.tensor_tensor(sc, ps_s[:, :].rearrange("p (h t) -> p h t", h=NH),
                                           q_var[:, q, :].unsqueeze(2).broadcast_to(full), ALU.mult), q, 1)
                    then(dve.tensor_tensor(sc, sc, mask_sb[:, q % 2, :].unsqueeze(1).broadcast_to(full),
                                           ALU.add), q, 2)
                    then(dve.tensor_reduce(s_max[:], sc, AX_X, ALU.max), q, 3)
                    then(dve.tensor_tensor(sc, sc, s_max[:].unsqueeze(2).broadcast_to(full),
                                           ALU.subtract), q, 4)

                def softmax_b(q):
                    sc = s[:, q % 2]
                    dve.wait_ge(exp_done, g * TPG + q + 1)
                    then(dve.tensor_reduce(s_sum[:], sc, AX_X, ALU.add), q, 5)
                    then(dve.reciprocal(s_sum[:], s_sum[:]), q, 6)
                    then(dve.tensor_tensor(sc, sc, s_sum[:].unsqueeze(2).broadcast_to(full),
                                           ALU.mult), q, 7)

                def o_low(q, b):
                    dve.wait_ge(o_hi_done, BASE + (g * TPG + q) * NB + b + 1)
                    hs = slice(b * HB, (b + 1) * HB)
                    dve.tensor_tensor(oT_lo[:, hs, :],
                                      bank(ps_o, b % 2).rearrange("p (h t) -> p h t", h=HB),
                                      oT_hi[:, hs, :].bitcast(F32), ALU.subtract).then_inc(o_lo_done, 1)

                softmax_a(0)
                softmax_b(0)
                for q in groups:
                    if q + 1 < TPG:
                        softmax_a(q + 1)
                    o_low(q, 0)
                    o_low(q, 1)
                    if q + 1 < TPG:
                        softmax_b(q + 1)
                    o_low(q, 2)
                    o_low(q, 3)
                    dve.wait_ge(out_ready, BASE + g * TPG + q + 1)
                    tile = xres[:, bass.ds(g * TPG + q, 1), :].rearrange("p a c -> p (a c)")
                    dve.tensor_tensor(tile, tile, ps_out[:, 0:HID], ALU.add).then_inc(out_added, 1)

        @block.tensor
        def _(pe):
            for sm in (xT_ready, k_ready, v_ready, q_ready, scores_ready, pT_ready, o_ready, out_ready):
                pe.sem_inc(sm, BASE)
            pe.wait_ge(small_loaded, 16 * 8)
            pe.wait_ge(consts_done, 2)
            with pe.Fori(0, NG) as g:
                for q in groups:
                    pe.wait_ge(normed, BASE + g * TPG + q + 1)
                    if q >= 2:
                        pe.wait_ge(xT_lo_done, BASE + g * TPG + q - 1)
                    else:
                        pe.wait_ge(pT_done, BASE + g * TPG)
                    for k in range(KK):
                        last = pe.transpose(bank(ps_q, q % 2)[:, k * P:(k + 1) * P],
                                            xn[:, q % 2, k * P:(k + 1) * P], ident)
                    last.then_inc(xT_ready, 1)
                pe.wait_ge(ctx_loaded, BASE + (g + 1) * 64)
                pe.wait_ge(out_added, BASE + g * TPG)
                for kv in range(NKV):
                    for k in range(KK):
                        last = pe.matmul(ps_out[:, kv * BG * SE:(kv + 1) * BG * SE],
                                         wk_sb[:, k, kv * D:(kv + 1) * D], cT[:, k, :, 0, :],
                                         start=k == 0, stop=k == KK - 1)
                last.then_inc(k_ready, 1)
                for hb in range(BG):
                    for k in range(KK):
                        last = pe.matmul(bank(ps_s, hb), cT[:, k, hb, :, :], wv_sb[:, k, :],
                                         start=k == 0, stop=k == KK - 1)
                    last.then_inc(v_ready, 1)

                def q_head(h):
                    if h >= 2:
                        pe.wait_ge(q_done, BASE + g * NH + h - 1)
                    cols = slice(h * D, (h + 1) * D)
                    terms = [(w[:, k, cols], a[:, k, :]) for k in range(KK)
                             for w, a in ((wq_hi, xT_hi), (wq_hi, xT_lo), (wq_lo, xT_hi))]
                    for m, (w, a) in enumerate(terms):
                        last = pe.matmul(bank(ps_q, h % 2), w, a, start=m == 0, stop=m == len(terms) - 1)
                    last.then_inc(q_ready, 1)

                def q_sum(h):
                    pe.wait_ge(q_squared, BASE + g * NH + h + 1)
                    for q in groups:
                        at = q * NH + h
                        last = pe.matmul(ps_ss[:, at:at + 1], q_sq[:, h % 2, q * P:(q + 1) * P],
                                         ones[:, 0:1], start=True, stop=True)
                    last.then_inc(q_summed, 1)

                pe.wait_ge(w_split, 1)
                pe.wait_ge(xT_lo_done, BASE + (g + 1) * TPG)
                for h in range(NH):
                    q_head(h)
                    if h == 0:
                        pe.wait_ge(k_squared, BASE + g + 1)
                        pe.matmul(bank(ps_o, 0), ones[:, :], k_sq[:].rearrange("p g t -> p (g t)"),
                                  start=True, stop=True).then_inc(k_summed, 1)
                    if h >= 2:
                        q_sum(h - 2)
                q_sum(NH - 2)
                q_sum(NH - 1)
                pe.wait_ge(k_done, g + 1)
                pe.wait_ge(v_done, BASE + (g + 1) * BG)
                pe.wait_ge(w_split, 2)

                def scores(q):
                    if q > 0:
                        pe.wait_ge(soft_step, BASE + (g * TPG + q - 1) * SOFT + 1)
                    hb = q // (TPG // BG)
                    for h in range(NH):
                        last = pe.matmul(ps_s[:, h * SE:(h + 1) * SE], qT[:, h, q * P:(q + 1) * P],
                                         kT[:, h // PER, hb * SE:(hb + 1) * SE], start=True, stop=True)
                    last.then_inc(scores_ready, 1)

                def values(q, b):
                    if q > 0 or b >= 2:
                        pe.wait_ge(o_lo_done, BASE + (g * TPG + q) * NB + b - 1)
                    hb = q // (TPG // BG)
                    for n, h in enumerate(heads_of(b)):
                        half = slice((h % 2) * SE, (h % 2 + 1) * SE)
                        last = pe.matmul(bank(ps_o, b % 2)[:, n * P:(n + 1) * P],
                                         v[half, hb, (h // PER) * D:(h // PER + 1) * D],
                                         pT[half, h // 2, :], start=True, stop=True)
                    last.then_inc(o_ready, 1)

                def project(q, b):
                    pe.wait_ge(o_lo_done, BASE + (g * TPG + q) * NB + b + 1)
                    if b == 0 and q > 0:
                        pe.wait_ge(out_added, BASE + g * TPG + q)
                    terms = [(a[:, b * HB + n, :], w[:, h, :]) for n, h in enumerate(heads_of(b))
                             for a, w in ((oT_hi, wo_hi), (oT_hi, wo_lo), (oT_lo, wo_hi))]
                    for m, (a, w) in enumerate(terms):
                        last = pe.matmul(ps_out[:, 0:HID], a, w, start=b == 0 and m == 0,
                                         stop=b == NB - 1 and m == len(terms) - 1)
                    if b == NB - 1:
                        last.then_inc(out_ready, 1)

                scores(0)
                for q in groups:
                    if q + 1 < TPG:
                        scores(q + 1)
                    pe.wait_ge(soft_step, BASE + (g * TPG + q + 1) * SOFT)
                    if q > 0:
                        pe.wait_ge(pT_done, BASE + g * TPG + q)
                    for n in range(NH // 2):
                        last = pe.transpose(ps_q[:, n * P:(n + 1) * P],
                                            s[:, q % 2, 2 * n:2 * n + 2, :].rearrange("p h t -> p (h t)"),
                                            ident)
                    last.then_inc(pT_ready, 1)
                    pe.wait_ge(pT_done, BASE + g * TPG + q + 1)
                    values(q, 0)
                    values(q, 1)
                    for b in range(NB):
                        project(q, b)
                        if b + 2 < NB:
                            values(q, b + 2)


def ffn_phase(nc, xres, ident, router_w, w_gate_up, w_down, out):
    E_ROUTED = router_w.shape[1] // KK
    E_ALL = w_down.shape[0]
    I = w_gate_up.shape[-1]
    IT = I // P
    UPE = NG
    PAIR = 2
    TURNS = E_ALL // PAIR
    UNITS = PAIR * UPE
    HT = UNITS * IT
    EPS = 1e-5
    RING = 2
    OUT0 = PAIR * NT

    with ExitStack() as ctx:
        def sb(name, shape, dt=F32):
            return ctx.enter_context(nc.sbuf_tensor(name, shape, dt))

        def sem(name):
            return ctx.enter_context(nc.semaphore(name))

        passed = sem("passed")

        st = sb("f_st", [P, NT, 6])
        mv = sb("f_mv", [P, NT, 2])
        veps = sb("f_veps", [P, NT])
        rstd = sb("f_rstd", [P, NT])
        neg_half = sb("f_neg_half", [P, NT])
        xn = sb("f_xn", [P, 2, HID])
        xT_hi = sb("f_xT_hi", [P, KK, TOK], F32R)
        xT_lo = sb("f_xT_lo", [P, KK, TOK], F32R)
        wr = sb("f_wr", [P, KK * E_ROUTED])
        wr_hi = sb("f_wr_hi", [P, KK, E_ROUTED], F32R)
        wr_lo = sb("f_wr_lo", [P, KK, E_ROUTED], F32R)
        score_e = sb("f_score_e", [P, NT, E_ROUTED])
        score = sb("f_score", [P, NT, E_ROUTED])
        above = sb("f_above", [P, NT, E_ROUTED, E_ROUTED])
        tied = sb("f_tied", [P, NT, E_ROUTED, E_ROUTED])
        earlier = sb("f_earlier", [P, E_ROUTED, E_ROUTED])
        rank = sb("f_rank", [P, NT, E_ROUTED])
        chosen = sb("f_chosen", [P, NT, E_ROUTED])
        total = sb("f_total", [P, NT])
        comb = sb("f_comb", [P, NT, E_ALL])
        wgu_raw = sb("f_wgu_raw", [P, 2, KK, I])
        wd_raw = sb("f_wd_raw", [P, IT, HID])
        wgu_hi = [sb(f"f_wgu_hi{b}", [P, 2, KK, I], F32R) for b in range(2)]
        wgu_lo = [sb(f"f_wgu_lo{b}", [P, 2, KK, I], F32R) for b in range(2)]
        wd_hi = [sb(f"f_wd_hi{b}", [P, IT, HID], F32R) for b in range(2)]
        wd_lo = [sb(f"f_wd_lo{b}", [P, IT, HID], F32R) for b in range(2)]
        silu = sb("f_silu", [P, 2, TG])
        h = sb("f_h", [P, 2, TG])
        h_hi = [sb(f"f_h_hi{b}", [P, IT, TG], F32R) for b in range(2)]
        h_lo = [sb(f"f_h_lo{b}", [P, IT, TG], F32R) for b in range(2)]

        ps = [ctx.enter_context(nc.psum_tensor(f"f_ps{i}", [P, TG], F32)) for i in range(8)]
        ps_gate, ps_up, ps_out = ps[0:2], ps[2:4], ps[4:8]
        ps_xT = ps[0:2]
        ps_logit = ps[2][:, 0:NT * E_ROUTED].rearrange("p (t e) -> p t e", t=NT)

        wr_loaded = sem("f_wr_loaded")
        weights_loaded = sem("f_weights_loaded")
        weights_copied = sem("f_weights_copied")
        weights_split = sem("f_weights_split")
        ln_stats = sem("f_ln_stats")
        ln_aggr = sem("f_ln_aggr")
        ln_veps = sem("f_ln_veps")
        ln_rstd = sem("f_ln_rstd")
        normed = sem("f_normed")
        xT_ready = sem("f_xT_ready")
        xT_hi_done = sem("f_xT_hi_done")
        xT_lo_done = sem("f_xT_lo_done")
        wr_done = sem("f_wr_done")
        consts_done = sem("f_consts_done")
        logits_ready = sem("f_logits_ready")
        score_exp = sem("f_score_exp")
        route_step = sem("f_route_step")
        gate_ready = sem("f_gate_ready")
        up_ready = sem("f_up_ready")
        silu_done = sem("f_silu_done")
        h_done = sem("f_h_done")
        h_hi_done = sem("f_h_hi_done")
        h_lo_done = sem("f_h_lo_done")
        out_ready = sem("f_out_ready")
        out_added = sem("f_out_added")
        stored = sem("f_stored")

        block = ctx.enter_context(nc.Block())

        @block.sync
        def _(sp):
            sp.dma_start(wr[:, :], router_w).then_inc(wr_loaded, 16)
            sp.dma_start(wgu_raw[:], w_gate_up[0]).then_inc(weights_loaded, 16)
            sp.dma_start(wd_raw[:], w_down[0]).then_inc(weights_loaded, 16)
            with sp.Fori(1, E_ALL) as e:
                sp.wait_ge(weights_split, 2 * e)
                sp.dma_start(wgu_raw[:], w_gate_up[e]).then_inc(weights_loaded, 16)
                sp.dma_start(wd_raw[:], w_down[e]).then_inc(weights_loaded, 16)
            out_t = out.rearrange("b (n p) c -> p (b n) c", p=P)
            for g in range(NG):
                sp.wait_ge(out_added, NT + E_ALL * NT - (NG - 1 - g) * TPG)
                ts = slice(g * TPG, (g + 1) * TPG)
                sp.dma_start(out_t[:, ts, :], xres[:, ts, :]).then_inc(stored, 16)
            sp.wait_ge(stored, 16 * NG)

        @block.gpsimd
        def _(pool):
            pool.memset(neg_half[:], -0.5).then_inc(consts_done, 1)
            pool.memset(earlier[:], 1.0).then_inc(consts_done, 1)
            pool.memset(comb[:], 1.0).then_inc(consts_done, 1)
            pool.wait_ge(consts_done, 3)
            pool.affine_select(out=earlier[:], in_=earlier[:], compare_op=ALU.is_gt, fill=0.0,
                               base=0, pattern=[[1, E_ROUTED], [-1, E_ROUTED]],
                               channel_multiplier=0).then_inc(consts_done, 1)
            pool.wait_ge(ln_aggr, 1)
            pool.tensor_scalar(veps[:], mv[:, :, 1], EPS, 0.0, ALU.add, ALU.add).then_inc(ln_veps, 1)
            pool.wait_ge(ln_veps, 1)
            pool.tensor_tensor(rstd[:], veps[:], neg_half[:], ALU.pow).then_inc(ln_rstd, 1)

            def split(e, b):
                pool.wait_ge(weights_loaded, 32 * e + 32)
                wait_apart(pool, out_ready, OUT0 + (e - 1) * NT, passed)
                for hi, raw in ((wgu_hi[b], wgu_raw), (wd_hi[b], wd_raw)):
                    pool.tensor_copy(hi[:], raw[:]).then_inc(weights_copied, 1)
                for n, (hi, lo, raw) in enumerate(((wgu_hi[b], wgu_lo[b], wgu_raw),
                                                   (wd_hi[b], wd_lo[b], wd_raw))):
                    wait_apart(pool, weights_copied, 2 * e + n + 1, passed)
                    pool.tensor_tensor(lo[:], raw[:], hi[:].bitcast(F32), ALU.subtract)\
                        .then_inc(weights_split, 1)

            with pool.Fori(0, TURNS) as turn:
                for b in range(PAIR):
                    split(turn * PAIR + b, b)

        @block.scalar
        def _(act):
            act.sem_inc(silu_done, RING)
            for n in range(NT):
                act.wait_ge(xT_ready, n + 1)
                act.activation(xT_hi[:, :, n * P:(n + 1) * P],
                               ps_xT[n % 2][:, 0:KK * P].rearrange("p (k t) -> p k t", k=KK),
                               ACT.Copy).then_inc(xT_hi_done, 1)
            act.wait_ge(route_step, 1)
            act.activation(score_e[:], score[:], ACT.Exp, scale=-1.0).then_inc(score_exp, 1)
            with act.Fori(0, TURNS) as turn:
                def to_hi(n):
                    u, it = n // IT, n % IT
                    act.wait_ge(h_done, RING + turn * HT + n + 1)
                    if it == 0:
                        act.wait_ge(out_ready, OUT0 + (turn * UNITS + u - 1) * TPG)
                    act.activation(h_hi[u % 2][:, it, :], h[:, n % 2, :], ACT.Copy)\
                        .then_inc(h_hi_done, 1)

                for n in range(HT):
                    act.wait_ge(gate_ready, turn * HT + n + 1)
                    act.wait_ge(h_done, turn * HT + n + 1)
                    act.activation(silu[:, n % 2, :], ps_gate[n % 2][:, :], ACT.Silu)\
                        .then_inc(silu_done, 1)
                    if n > 0:
                        to_hi(n - 1)
                to_hi(HT - 1)

        @block.vector
        def _(dve):
            dve.sem_inc(h_done, RING)
            dve.sem_inc(h_lo_done, RING)
            dve.sem_inc(out_added, NT)
            layernorm_stats_steps(dve, st, mv, lambda t: xres[:, t, :], range(NT),
                                  ln_stats, ln_aggr, 0)
            dve.wait_ge(wr_loaded, 16)
            dve.tensor_copy(wr_hi[:], wr[:]).then_inc(wr_done, 1)
            dve.wait_ge(wr_done, 1)
            dve.tensor_tensor(wr_lo[:], wr[:].rearrange("p (k e) -> p k e", k=KK),
                              wr_hi[:].bitcast(F32), ALU.subtract).then_inc(wr_done, 1)
            dve.wait_ge(ln_rstd, 1)

            def xT_low(n):
                dve.wait_ge(xT_hi_done, n + 1)
                ts = slice(n * P, (n + 1) * P)
                dve.tensor_tensor(xT_lo[:, :, ts],
                                  ps_xT[n % 2][:, 0:KK * P].rearrange("p (k t) -> p k t", k=KK),
                                  xT_hi[:, :, ts].bitcast(F32), ALU.subtract).then_inc(xT_lo_done, 1)

            for n in range(NT):
                if n >= 2:
                    dve.wait_ge(xT_ready, n - 1)
                dve.tensor_scalar(xn[:, n % 2, :], xres[:, n, :], mv[:, n, 0:1], rstd[:, n:n + 1],
                                  ALU.subtract, ALU.mult).then_inc(normed, 1)
                if n > 0:
                    xT_low(n - 1)
            xT_low(NT - 1)

            step = [0]

            def then(ins):
                step[0] += 1
                ins.then_inc(route_step, 1)
                dve.wait_ge(route_step, step[0])

            dve.wait_ge(consts_done, 4)
            dve.wait_ge(logits_ready, 1)
            then(dve.tensor_scalar(score[:], ps_logit, -88.0, None, ALU.max))
            dve.wait_ge(score_exp, 1)
            then(dve.tensor_scalar(score[:], score_e[:], 1.0, None, ALU.add))
            then(dve.reciprocal(score[:], score[:]))
            shape = [P, NT, E_ROUTED, E_ROUTED]
            mine = score[:].unsqueeze(3).broadcast_to(shape)
            other = score[:].unsqueeze(2).broadcast_to(shape)
            dve.tensor_tensor(above[:], other, mine, ALU.is_gt)
            then(dve.tensor_tensor(tied[:], other, mine, ALU.is_equal))
            then(dve.tensor_tensor(tied[:], tied[:], earlier[:].unsqueeze(1).broadcast_to(shape),
                                   ALU.mult))
            then(dve.tensor_tensor(above[:], above[:], tied[:], ALU.add))
            then(dve.tensor_reduce(rank[:], above[:], AX_X, ALU.add))
            then(dve.scalar_tensor_tensor(out=chosen[:], in0=rank[:], scalar=1.5, in1=score[:],
                                          op0=ALU.is_lt, op1=ALU.mult))
            then(dve.tensor_reduce(total[:], chosen[:], AX_X, ALU.add))
            then(dve.reciprocal(total[:], total[:]))
            then(dve.tensor_tensor(comb[:, :, 0:E_ROUTED], chosen[:],
                                   total[:].unsqueeze(2).broadcast_to([P, NT, E_ROUTED]), ALU.mult))

            with dve.Fori(0, TURNS) as turn:
                def to_lo(n):
                    u, it = n // IT, n % IT
                    dve.wait_ge(h_hi_done, turn * HT + n + 1)
                    dve.tensor_tensor(h_lo[u % 2][:, it, :], h[:, n % 2, :],
                                      h_hi[u % 2][:, it, :].bitcast(F32), ALU.subtract)\
                        .then_inc(h_lo_done, 1)

                def add(u):
                    for q in range(TPG):
                        t = (u % UPE) * TPG + q
                        dve.wait_ge(out_ready, OUT0 + (turn * UNITS + u) * TPG + q + 1)
                        dve.wait_ge(out_added, turn * UNITS * TPG + u * TPG + q + 1)
                        dve.scalar_tensor_tensor(
                            out=xres[:, t, :], in0=ps_out[q][:, 0:HID],
                            scalar=comb[:, t, bass.ds(turn * PAIR + u // UPE, 1)],
                            in1=xres[:, t, :], op0=ALU.mult, op1=ALU.add).then_inc(out_added, 1)

                for u in range(UNITS):
                    for n in range(u * IT, (u + 1) * IT):
                        dve.wait_ge(silu_done, RING + turn * HT + n + 1)
                        dve.wait_ge(up_ready, turn * HT + n + 1)
                        dve.wait_ge(h_lo_done, turn * HT + n + 1)
                        dve.tensor_tensor(h[:, n % 2, :], silu[:, n % 2, :],
                                          ps_up[n % 2][:, :], ALU.mult).then_inc(h_done, 1)
                        if n > 0:
                            to_lo(n - 1)
                    if u > 0:
                        add(u - 1)
                to_lo(HT - 1)
                add(UNITS - 1)

        @block.tensor
        def _(pe):
            for n in range(NT):
                pe.wait_ge(normed, n + 1)
                if n >= 2:
                    pe.wait_ge(xT_lo_done, n - 1)
                for k in range(KK):
                    last = pe.transpose(ps_xT[n % 2][:, k * P:(k + 1) * P],
                                        xn[:, n % 2, k * P:(k + 1) * P], ident)
                last.then_inc(xT_ready, 1)
            pe.wait_ge(xT_lo_done, NT)
            pe.wait_ge(wr_done, 2)
            for n in range(NT):
                ts = slice(n * P, (n + 1) * P)
                terms = [(a[:, k, ts], w[:, k, :]) for k in range(KK)
                         for a, w in ((xT_hi, wr_hi), (xT_hi, wr_lo), (xT_lo, wr_hi))]
                for m, (a, w) in enumerate(terms):
                    last = pe.matmul(ps_logit[:, n, :], a, w, start=m == 0, stop=m == len(terms) - 1)
            last.then_inc(logits_ready, 1)
            pe.wait_ge(route_step, 1)
            pe.sem_inc(out_ready, OUT0)

            with pe.Fori(0, TURNS) as turn:
                def gate_up(u):
                    b, ts = u // UPE, slice((u % UPE) * TG, (u % UPE + 1) * TG)
                    if u % UPE == 0:
                        pe.wait_ge(weights_split, turn * PAIR * 2 + 2 * b + 2)
                    for it in range(IT):
                        n = u * IT + it
                        for g, (bank, free, ready) in enumerate(((ps_gate, silu_done, gate_ready),
                                                                 (ps_up, h_done, up_ready))):
                            pe.wait_ge(free, turn * HT + n + 1)
                            cols = slice(it * P, (it + 1) * P)
                            terms = [(w[:, g, k, cols], a[:, k, ts]) for k in range(KK)
                                     for w, a in ((wgu_hi[b], xT_hi), (wgu_hi[b], xT_lo),
                                                  (wgu_lo[b], xT_hi))]
                            for m, (w, a) in enumerate(terms):
                                last = pe.matmul(bank[n % 2][:, :], w, a, start=m == 0,
                                                 stop=m == len(terms) - 1)
                            last.then_inc(ready, 1)

                def down(u):
                    b = u // UPE
                    pe.wait_ge(h_lo_done, RING + turn * HT + (u + 1) * IT)
                    for q in range(TPG):
                        pe.wait_ge(out_added, NT - TPG + (turn * UNITS + u) * TPG + q + 1)
                        terms = [(a[:, it, q * P:(q + 1) * P], w[:, it, :]) for it in range(IT)
                                 for a, w in ((h_hi[u % 2], wd_hi[b]), (h_hi[u % 2], wd_lo[b]),
                                              (h_lo[u % 2], wd_hi[b]))]
                        for m, (a, w) in enumerate(terms):
                            last = pe.matmul(ps_out[q][:, 0:HID], a, w, start=m == 0,
                                             stop=m == len(terms) - 1)
                        last.then_inc(out_ready, 1)

                for u in range(UNITS):
                    gate_up(u)
                    if u > 0:
                        down(u - 1)
                down(UNITS - 1)


def decoder_layer(nc, x, w_xz, w_bc, w_dt, conv_w, conv_b, dt_bias, a_log, d_param, norm_w, w_out,
                  ctx_T, mask, wq, bq, wk, bk, wv, bv, wo, qn, kn, router_w, w_gate_up, w_down, out):
    with ExitStack() as ctx:
        xres = ctx.enter_context(nc.sbuf_tensor("xres", [P, NT, HID], F32))
        ident = ctx.enter_context(nc.sbuf_tensor("ident", [P, P], F32))
        ident_done = ctx.enter_context(nc.semaphore("ident_done"))
        with nc.Block() as block:
            @block.gpsimd
            def _(pool):
                pool.memset(ident[:], 0.0).then_inc(ident_done, 1)
                pool.wait_ge(ident_done, 1)
                pool.affine_select(out=ident[:], in_=ident[:], compare_op=ALU.not_equal, fill=1.0, base=0,
                                   pattern=[[-1, P]], channel_multiplier=1).then_inc(ident_done, 1)
                pool.wait_ge(ident_done, 2)
        mamba_phase(nc, xres, ident[:], x, w_xz, w_bc, w_dt, conv_w, conv_b, dt_bias, a_log, d_param,
                    norm_w, w_out)
        cross_attention_phase(nc, xres, ident[:], ctx_T, mask, wq, bq, wk, bk, wv, bv, wo, qn, kn)
        ffn_phase(nc, xres, ident[:], router_w, w_gate_up, w_down, out)


def lay_out(i):
    import numpy as np

    def tiled(w):
        return w.reshape(-1, KK, P).transpose(2, 1, 0)

    w_in = i["L0_attn_W_in"]
    inner = i["L0_attn_W_out"].shape[1]
    nct, heads = inner // P, i["L0_attn_D_param"].shape[0]
    z, xx = (w_in[n * inner:(n + 1) * inner].reshape(nct, P, KK, P) for n in range(2))
    bc = w_in[2 * inner:w_in.shape[0] - heads]
    gate_up = np.concatenate([np.stack([i["L0_ffn_wg"], i["L0_ffn_wu"]], 1),
                              np.stack([i["L0_ffn_sg"], i["L0_ffn_su"]], 1)], 0)
    down = np.concatenate([i["L0_ffn_wd"], i["L0_ffn_sd"]], 0)
    e, _, width, _ = gate_up.shape
    q_heads = i["L0_xattn_Wq"].shape[1] // P
    kv_heads = i["L0_xattn_Wk"].shape[1] // P
    context = i["ctx_2048"].shape[1]
    out = {
        "x": i["x"],
        "w_xz": np.stack([xx, z], 0).transpose(1, 4, 0, 3, 2),
        "w_bc": tiled(bc),
        "w_dt": tiled(w_in[w_in.shape[0] - heads:]),
        "conv_w": i["L0_attn_conv_w"].reshape(-1, P, i["L0_attn_conv_w"].shape[-1]).transpose(1, 0, 2),
        "conv_b": i["L0_attn_conv_b"].reshape(-1, P).T,
        "dt_bias": i["L0_attn_dt_bias"],
        "a_log": i["L0_attn_A_log"],
        "d_param": i["L0_attn_D_param"].reshape(nct, heads // nct).T,
        "norm_w": i["L0_attn_norm_w"].reshape(nct, P).T,
        "w_out": i["L0_attn_W_out"].reshape(HID, nct, P).transpose(1, 2, 0),
        "ctx_T": i["ctx_2048"].reshape(NG, -1, context, KK, P).transpose(0, 4, 3, 1, 2),
        "mask": i["mask_1xSxS2_ff0"].reshape(-1, P, context).transpose(1, 0, 2),
        "wq": i["L0_xattn_Wq"].reshape(KK, P, -1).transpose(1, 0, 2),
        "bq": i["L0_xattn_bq"].reshape(q_heads, P).T,
        "wk": i["L0_xattn_Wk"].reshape(KK, P, -1).transpose(1, 0, 2),
        "bk": i["L0_xattn_bk"].reshape(kv_heads, P).T,
        "wv": i["L0_xattn_Wv"].reshape(KK, P, -1).transpose(1, 0, 2),
        "bv": i["L0_xattn_bv"],
        "wo": i["L0_xattn_Wo"].reshape(q_heads, P, HID).transpose(1, 0, 2).reshape(P, -1),
        "qn": i["L0_xattn_qn_w"].reshape(P, 1),
        "kn": i["L0_xattn_kn_w"].reshape(P, 1),
        "router_w": i["L0_ffn_w_router"].reshape(-1, KK, P).transpose(2, 1, 0).reshape(P, -1),
        "w_gate_up": gate_up.reshape(e, 2, width, KK, P).transpose(0, 4, 1, 3, 2),
        "w_down": down.reshape(e, HID, width // P, P).transpose(0, 3, 2, 1),
    }
    return {name: np.ascontiguousarray(a) for name, a in out.items()}


def kernel(**inputs):
    import numpy as np
    import concourse.bacc as bacc
    from concourse.bass_utils import run_bass_kernel_spmd

    arrays = lay_out({name: np.asarray(a) for name, a in inputs.items()})
    nc = bacc.Bacc("TRN2", target_bir_lowering=False, num_devices=1)
    args = {name: nc.dram_tensor("in_" + name, a.shape, mybir.dt.from_np(a.dtype), kind="ExternalInput").ap()
            for name, a in arrays.items()}
    shape = inputs["x"].shape
    args["out"] = nc.dram_tensor("out", shape, F32, kind="ExternalOutput").ap()
    decoder_layer(nc, **args)
    r = run_bass_kernel_spmd(nc, [{"in_" + name: a for name, a in arrays.items()}], core_ids=[0])
    return r.results[0]["out"]
```
